# Optimizing a Trainium2 kernel written in Bass

```python
import numpy as np
import jax
import jax.numpy as jnp

def _softmax(x, axis=-1):
    return jax.nn.softmax(x, axis=axis)

def _gelu(x):
    return jax.nn.gelu(x, approximate=True)

def _silu(x):
    return jax.nn.silu(x)

def _sigmoid(x):
    return jax.nn.sigmoid(x)

def _layernorm(x, axis=-1, eps=1e-05):
    m = jnp.mean(x, axis=axis, keepdims=True)
    v = jnp.var(x, axis=axis, keepdims=True)
    return (x - m) / jnp.sqrt(v + eps)

def _scatter_add(tgt, idx, src, axis=0):
    return tgt.at[idx].add(src)

def _segment_sum(src, seg, n):
    return jax.ops.segment_sum(src, seg, n)
kernel_name = 'mk_gnn_resnorm_d4_gnn_r8_725115'

def setup_inputs(seed: int=0):
    np.random.seed(seed)
    _w = jnp.asarray

    def _rec_inputs():
        import jax
        import jax.numpy as jnp
        _gk = jax.random.key(seed)
        x = -0.0003713 + 1 * jax.random.normal(jax.random.fold_in(_gk, 1), (12500, 128), jnp.float32)
        src = jax.random.randint(jax.random.fold_in(_gk, 2), (200000,), 0, 12500, jnp.int32)
        dst = jax.random.randint(jax.random.fold_in(_gk, 3), (200000,), 0, 12500, jnp.int32)
        _o = jnp.argsort(dst, stable=True)
        src = src[_o]
        dst = dst[_o]
        edge_weight = jax.random.uniform(jax.random.fold_in(_gk, 13), (200000,), jnp.float32, 0.0, 0.999998)
        return (x, src, dst, edge_weight)
    x, src, dst, edge_weight = _rec_inputs()

    def _L0_gnn_setup():
        import jax, jax.numpy as jnp
        import numpy as np
        N_NODES = 12500
        N_INCID = 250000
        HIDDEN = 128
        N_HE = 12500
        key = jax.random.key(seed)
        k1, k2, k3 = jax.random.split(key, 3)
        node_feats = jax.random.normal(k1, (N_NODES, HIDDEN), dtype=jnp.float32)
        hyperedge_index = jax.random.randint(k2, (2, N_INCID), 0, N_HE, dtype=jnp.int64)
        bound = float(np.sqrt(6.0 / (HIDDEN + 1)))
        W = jax.random.uniform(k3, (1, HIDDEN), dtype=jnp.float32, minval=-bound, maxval=bound)
        return {'node_feats': node_feats, 'hyperedge_index': hyperedge_index, 'num_hyperedges': N_HE, 'W': W}
    _L0_gnn_all = _L0_gnn_setup()
    _L0_gnn_in = {k: v for k, v in _L0_gnn_all.items() if k in ('W',)}
    del _L0_gnn_all

    def _L1_gnn_setup():
        import jax, jax.numpy as jnp
        import numpy as np
        LEAKY_SLOPE = 0.2
        N_NODES = 6250
        N_EDGES = 100000
        IN_DIM = 128
        OUT_DIM = 64
        HEADS = 4
        MLP_HID = 256
        MLP_OUT = 128

        def _gat_forward(node_embeddings, src, dst, W_n, a_src, a_dst, mlp_W1, mlp_b1, mlp_W2, mlp_b2):
            N = node_embeddings.shape[0]
            h = jnp.einsum('nc,hcd->nhd', node_embeddings, W_n)
            s_src = jnp.einsum('nhd,hd->nh', h, a_src)
            s_dst = jnp.einsum('nhd,hd->nh', h, a_dst)
            e = jax.nn.leaky_relu(s_src[src] + s_dst[dst], negative_slope=LEAKY_SLOPE)
            e_max = jax.ops.segment_max(e, dst, num_segments=N)
            ex = jnp.exp(e - e_max[dst])
            den = jax.ops.segment_sum(ex, dst, num_segments=N)
            m = h[src]
            num = jax.ops.segment_sum(ex[:, :, None] * m, dst, num_segments=N)
            safe_den = jnp.where(den > 0, den, 1.0)
            head_out = jax.nn.relu(num / safe_den[:, :, None])
            concat = head_out.reshape(N, -1)
            hidden = jax.nn.relu(concat @ mlp_W1 + mlp_b1)
            return hidden @ mlp_W2 + mlp_b2
        key = jax.random.key(seed)
        ks = jax.random.split(key, 10)
        node_embeddings = jax.random.normal(ks[0], (N_NODES, IN_DIM), dtype=jnp.float32)
        src = jax.random.randint(ks[1], (N_EDGES,), 0, N_NODES, dtype=jnp.int32)
        dst = jax.random.randint(ks[2], (N_EDGES,), 0, N_NODES, dtype=jnp.int32)
        W_n = jax.random.normal(ks[3], (HEADS, IN_DIM, OUT_DIM), dtype=jnp.float32) * (1.0 / np.sqrt(IN_DIM))
        a_src = jax.random.normal(ks[4], (HEADS, OUT_DIM), dtype=jnp.float32) * (1.0 / np.sqrt(OUT_DIM))
        a_dst = jax.random.normal(ks[5], (HEADS, OUT_DIM), dtype=jnp.float32) * (1.0 / np.sqrt(OUT_DIM))
        mlp_W1 = jax.random.normal(ks[6], (HEADS * OUT_DIM, MLP_HID), dtype=jnp.float32) * (1.0 / np.sqrt(HEADS * OUT_DIM))
        mlp_b1 = jnp.zeros((MLP_HID,), dtype=jnp.float32)
        mlp_W2 = jax.random.normal(ks[7], (MLP_HID, MLP_OUT), dtype=jnp.float32) * (1.0 / np.sqrt(MLP_HID))
        mlp_b2 = jnp.zeros((MLP_OUT,), dtype=jnp.float32)
        return {'node_embeddings': node_embeddings, 'src': src, 'dst': dst, 'W_n': W_n, 'a_src': a_src, 'a_dst': a_dst, 'mlp_W1': mlp_W1, 'mlp_b1': mlp_b1, 'mlp_W2': mlp_W2, 'mlp_b2': mlp_b2}
    _L1_gnn_all = _L1_gnn_setup()
    _L1_gnn_in = {k: v for k, v in _L1_gnn_all.items() if k in ('W_n', 'a_src', 'a_dst', 'mlp_W1', 'mlp_b1', 'mlp_W2', 'mlp_b2')}
    del _L1_gnn_all

    def _L2_gnn_setup():
        import jax, jax.numpy as jnp
        import numpy as np
        N_NODES = 6250
        N_EDGES = 100000
        IN_FEAT = 128
        OUT_FEAT = 128
        key = jax.random.key(seed)
        k1, k2, k3 = jax.random.split(key, 3)
        x = jax.random.normal(k1, (N_NODES, IN_FEAT), dtype=jnp.float32)
        edge_index = jax.random.randint(k2, (2, N_EDGES), 0, N_NODES, dtype=jnp.int32)
        limit = np.sqrt(6.0 / (IN_FEAT + OUT_FEAT)).astype(np.float32)
        W = jax.random.uniform(k3, (IN_FEAT, OUT_FEAT), minval=-limit, maxval=limit, dtype=jnp.float32)
        b = jnp.zeros((OUT_FEAT,), dtype=jnp.float32)
        return {'x': x, 'edge_index': edge_index, 'W': W, 'b': b}
    _L2_gnn_all = _L2_gnn_setup()
    _L2_gnn_in = {k: v for k, v in _L2_gnn_all.items() if k in ('W', 'b')}
    del _L2_gnn_all

    def _L3_gnn_setup():
        import jax, jax.numpy as jnp
        import numpy as np
        HID = 128
        N_NODES = 6250
        N_EDGES = 75000

        def _layernorm(x, gamma, beta, eps=1e-05):
            mu = jnp.mean(x, axis=-1, keepdims=True)
            var = jnp.var(x, axis=-1, keepdims=True)
            return (x - mu) * jax.lax.rsqrt(var + eps) * gamma + beta
        key = jax.random.key(seed)
        ks = jax.random.split(key, 12)
        d = HID
        s = lambda fan_in: 1.0 / np.sqrt(fan_in)
        return {'hidden': jax.random.normal(ks[0], (N_NODES, d), dtype=jnp.float32), 'edge_index': jax.random.randint(ks[1], (2, N_EDGES), 0, N_NODES, dtype=jnp.int32), 'edge_weight': jax.random.uniform(ks[2], (N_EDGES,), dtype=jnp.float32), 'We1': jax.random.uniform(ks[3], (2 * d + 1, d), jnp.float32, -s(2 * d + 1), s(2 * d + 1)), 'be1': jnp.zeros((d,), jnp.float32), 'We2': jax.random.uniform(ks[4], (d, d), jnp.float32, -s(d), s(d)), 'be2': jnp.zeros((d,), jnp.float32), 'Wu1': jax.random.uniform(ks[5], (2 * d, d), jnp.float32, -s(2 * d), s(2 * d)), 'bu1': jnp.zeros((d,), jnp.float32), 'Wu2': jax.random.uniform(ks[6], (d, d), jnp.float32, -s(d), s(d)), 'bu2': jnp.zeros((d,), jnp.float32), 'gamma': jnp.ones((d,), jnp.float32), 'beta': jnp.zeros((d,), jnp.float32)}
    _L3_gnn_all = _L3_gnn_setup()
    _L3_gnn_in = {k: v for k, v in _L3_gnn_all.items() if k in ('We1', 'be1', 'We2', 'be2', 'Wu1', 'bu1', 'Wu2', 'bu2', 'gamma', 'beta')}
    del _L3_gnn_all
    return {'x': x, 'src': src, 'dst': dst, 'edge_weight': edge_weight, 'L0_gnn_W': _L0_gnn_in['W'], 'L1_gnn_W_n': _L1_gnn_in['W_n'], 'L1_gnn_a_src': _L1_gnn_in['a_src'], 'L1_gnn_a_dst': _L1_gnn_in['a_dst'], 'L1_gnn_mlp_W1': _L1_gnn_in['mlp_W1'], 'L1_gnn_mlp_b1': _L1_gnn_in['mlp_b1'], 'L1_gnn_mlp_W2': _L1_gnn_in['mlp_W2'], 'L1_gnn_mlp_b2': _L1_gnn_in['mlp_b2'], 'L2_gnn_W': _L2_gnn_in['W'], 'L2_gnn_b': _L2_gnn_in['b'], 'L3_gnn_We1': _L3_gnn_in['We1'], 'L3_gnn_be1': _L3_gnn_in['be1'], 'L3_gnn_We2': _L3_gnn_in['We2'], 'L3_gnn_be2': _L3_gnn_in['be2'], 'L3_gnn_Wu1': _L3_gnn_in['Wu1'], 'L3_gnn_bu1': _L3_gnn_in['bu1'], 'L3_gnn_Wu2': _L3_gnn_in['Wu2'], 'L3_gnn_bu2': _L3_gnn_in['bu2'], 'L3_gnn_gamma': _L3_gnn_in['gamma'], 'L3_gnn_beta': _L3_gnn_in['beta']}

def reference(x, src, dst, edge_weight, L0_gnn_W, L1_gnn_W_n, L1_gnn_a_src, L1_gnn_a_dst, L1_gnn_mlp_W1, L1_gnn_mlp_b1, L1_gnn_mlp_W2, L1_gnn_mlp_b2, L2_gnn_W, L2_gnn_b, L3_gnn_We1, L3_gnn_be1, L3_gnn_We2, L3_gnn_be2, L3_gnn_Wu1, L3_gnn_bu1, L3_gnn_Wu2, L3_gnn_bu2, L3_gnn_gamma, L3_gnn_beta):
    import jax
    import jax.numpy as jnp

    def _L0_gnn_ref(node_feats, hyperedge_index, num_hyperedges, W):
        import jax, jax.numpy as jnp
        import numpy as np
        N_NODES = 12500
        N_INCID = 250000
        HIDDEN = 128
        N_HE = 12500
        node_idx = hyperedge_index[0]
        he_idx = hyperedge_index[1]
        gathered = node_feats[node_idx]
        scores = jnp.einsum('ed,d->e', gathered, W[0])
        seg_max = jax.ops.segment_max(scores, he_idx, num_segments=num_hyperedges)
        seg_max = jnp.where(jnp.isfinite(seg_max), seg_max, 0.0)
        w = jnp.exp(scores - seg_max[he_idx])
        denom = jax.ops.segment_sum(w, he_idx, num_segments=num_hyperedges)
        w_norm = w / jnp.maximum(denom, 1e-20)[he_idx]
        out = jax.ops.segment_sum(w_norm[:, None] * gathered, he_idx, num_segments=num_hyperedges)
        return out

    def _L1_gnn_ref(node_embeddings, src, dst, W_n, a_src, a_dst, mlp_W1, mlp_b1, mlp_W2, mlp_b2):
        import jax, jax.numpy as jnp
        import numpy as np
        LEAKY_SLOPE = 0.2
        N_NODES = 6250
        N_EDGES = 100000
        IN_DIM = 128
        OUT_DIM = 64
        HEADS = 4
        MLP_HID = 256
        MLP_OUT = 128

        def _gat_forward(node_embeddings, src, dst, W_n, a_src, a_dst, mlp_W1, mlp_b1, mlp_W2, mlp_b2):
            N = node_embeddings.shape[0]
            h = jnp.einsum('nc,hcd->nhd', node_embeddings, W_n)
            s_src = jnp.einsum('nhd,hd->nh', h, a_src)
            s_dst = jnp.einsum('nhd,hd->nh', h, a_dst)
            e = jax.nn.leaky_relu(s_src[src] + s_dst[dst], negative_slope=LEAKY_SLOPE)
            e_max = jax.ops.segment_max(e, dst, num_segments=N)
            ex = jnp.exp(e - e_max[dst])
            den = jax.ops.segment_sum(ex, dst, num_segments=N)
            m = h[src]
            num = jax.ops.segment_sum(ex[:, :, None] * m, dst, num_segments=N)
            safe_den = jnp.where(den > 0, den, 1.0)
            head_out = jax.nn.relu(num / safe_den[:, :, None])
            concat = head_out.reshape(N, -1)
            hidden = jax.nn.relu(concat @ mlp_W1 + mlp_b1)
            return hidden @ mlp_W2 + mlp_b2
        return _gat_forward(node_embeddings, src, dst, W_n, a_src, a_dst, mlp_W1, mlp_b1, mlp_W2, mlp_b2)

    def _L2_gnn_ref(x, edge_index, W, b):
        import jax, jax.numpy as jnp
        import numpy as np
        N_NODES = 6250
        N_EDGES = 100000
        IN_FEAT = 128
        OUT_FEAT = 128
        n = x.shape[0]
        loops = jnp.arange(n, dtype=edge_index.dtype)
        src = jnp.concatenate([edge_index[0], loops])
        dst = jnpp_concat = jnp.concatenate([edge_index[1], loops])
        deg = jax.ops.segment_sum(jnp.ones_like(dst, dtype=x.dtype), dst, num_segments=n)
        dinv = jnp.where(deg > 0, jax.lax.rsqrt(deg), 0.0)
        norm = dinv[src] * dinv[dst]
        h = x @ W
        msgs = h[src] * norm[:, None]
        out = jax.ops.segment_sum(msgs, dst, num_segments=n) + b
        return jax.nn.gelu(out, approximate=False)

    def _L3_gnn_ref(hidden, edge_index, edge_weight, We1, be1, We2, be2, Wu1, bu1, Wu2, bu2, gamma, beta):
        import jax, jax.numpy as jnp
        import numpy as np
        HID = 128
        N_NODES = 6250
        N_EDGES = 75000

        def _layernorm(x, gamma, beta, eps=1e-05):
            mu = jnp.mean(x, axis=-1, keepdims=True)
            var = jnp.var(x, axis=-1, keepdims=True)
            return (x - mu) * jax.lax.rsqrt(var + eps) * gamma + beta
        src, dst = (edge_index[0], edge_index[1])
        edge_inputs = jnp.concatenate([hidden[src], hidden[dst], edge_weight[:, None]], axis=1)
        h = jax.nn.gelu(edge_inputs @ We1 + be1, approximate=False)
        messages = h @ We2 + be2
        aggregated = jax.ops.segment_sum(messages, dst, num_segments=hidden.shape[0])
        u = jnp.concatenate([hidden, aggregated], axis=1)
        u = jax.nn.gelu(u @ Wu1 + bu1, approximate=False)
        updated = u @ Wu2 + bu2
        return _layernorm(hidden + updated, gamma, beta)
    edge_index = jnp.stack([src, dst])
    x = _layernorm(x + _L0_gnn_ref(x, edge_index, 12500, L0_gnn_W), axis=-1)
    x = _layernorm(x + _L1_gnn_ref(x, src, dst, L1_gnn_W_n, L1_gnn_a_src, L1_gnn_a_dst, L1_gnn_mlp_W1, L1_gnn_mlp_b1, L1_gnn_mlp_W2, L1_gnn_mlp_b2), axis=-1)
    x = _layernorm(x + _L2_gnn_ref(x, edge_index, L2_gnn_W, L2_gnn_b), axis=-1)
    x = _layernorm(x + _L3_gnn_ref(x, edge_index, edge_weight, L3_gnn_We1, L3_gnn_be1, L3_gnn_We2, L3_gnn_be2, L3_gnn_Wu1, L3_gnn_bu1, L3_gnn_Wu2, L3_gnn_bu2, L3_gnn_gamma, L3_gnn_beta), axis=-1)
    return x

_drawn_inputs = setup_inputs


def setup_inputs(seed=0):
    import zlib

    import numpy as np

    out = dict(_drawn_inputs(seed))
    spreads = {'L1_gnn_mlp_b1': (0.0, 0.1),
     'L1_gnn_mlp_b2': (0.0, 0.1),
     'L2_gnn_b': (0.0, 0.1),
     'L3_gnn_be1': (0.0, 0.1),
     'L3_gnn_be2': (0.0, 0.1),
     'L3_gnn_bu1': (0.0, 0.413),
     'L3_gnn_bu2': (0.0, 0.1),
     'L3_gnn_gamma': (1.0, 0.2),
     'L3_gnn_beta': (0.0, 0.1)}
    factors = {'edge_weight': 53.035}
    for name, (base, spread) in spreads.items():
        noise = np.random.default_rng([zlib.crc32(name.encode()), seed]).standard_normal(out[name].shape)
        drawn = base * np.exp(spread * noise) if base else spread * noise
        out[name] = jnp.asarray(drawn.astype(out[name].dtype))
    for name, factor in factors.items():
        out[name] = (out[name] * factor).astype(out[name].dtype)
    return out
```

```python
from contextlib import ExitStack

import concourse.bass as bass
from concourse import mybir

F32 = mybir.dt.float32
BF16 = mybir.dt.bfloat16
I32 = mybir.dt.int32
U8 = mybir.dt.uint8
ALU = mybir.AluOpType
ACT = mybir.ActivationFunctionType
AX = mybir.AxisListType

P = 128
N = 12500
F = 128
E = 200000
H = 4
DH = 64
NT = -(-N // P)
NP = NT * P
NLAST = N - (NT - 1) * P
NB = 16
EB = NB * P
B = -(-E // EB)
ELAST = E - (B - 1) * EB
PAD_NODE = NP - 1
RANKS = N + 4 * P + 4
DRANKS = NP + 2 * P
BIG = 1.0e30
G = 7
NG = NT // G
META = 5
W0, W1 = F + 1, H * DH + H
assert NT % G == 0 and (B - 2) % 6 == 0 and B <= P


def one_hot(eng, out, iota, index, weight=None):
    if weight is None:
        return eng.tensor_scalar(out, iota, index, None, ALU.is_equal)
    return eng.tensor_scalar(out, iota, index, weight, ALU.is_equal, ALU.mult)


def prog(nc, a, out, stop=99, debug=False):
    kind = "ExternalOutput" if debug else "Internal"

    def dram(name, shape, dt):
        return nc.dram_tensor(name, shape, dt, kind=kind).ap()

    meta_d = dram("meta_d", (B, P, META, NB), F32)
    pen_d = dram("pen_d", (B, NB, P + 1), F32)
    rowpen_d = dram("rowpen_d", (B, 2, H * (NB + 1)), F32)
    lrrow_d = dram("lrrow_d", (B, EB), U8)
    base_d = dram("base_d", (B, NB), I32)
    rel_d = dram("rel_d", (B, NB), I32)
    qbase_d = dram("qbase_d", (B, NB // 4), I32)
    wflat_d = dram("wflat_d", (B, EB), F32)
    t0_d = dram("t0_d", (NP, W0), F32)
    t1_d = dram("t1_d", (NP, W1), F32)
    t2_d = dram("t2_d", (NP, F), F32)
    t3_d = dram("t3_d", (NP, F), F32)
    x_d = dram("x_d", (NP, F), F32)
    sd_d = dram("sd_d", (DRANKS, 3 * H), BF16)
    bd_d = dram("bd_d", (DRANKS, F), F32)
    rb_d = dram("rb_d", (NT, 1), I32)
    deg_d = dram("deg_d", (NT, P), F32)

    with ExitStack() as top:
        def sb(name, shape, dt=F32, ctx=top):
            return ctx.enter_context(nc.sbuf_tensor(name, shape, dt))

        iota = sb("iota", [P, P])
        iotab = sb("iotab", [P, P], BF16)
        iotap = sb("iotap", [P, 1])
        ident = sb("ident", [P, P])
        ones = sb("ones", [P, P])
        lrn = sb("lrn", [P, NT])
        grank = sb("grank", [P, NT])
        dinv = sb("dinv", [P, NT])

        with ExitStack() as ctx:
            def s(name, shape, dt=F32):
                return sb(name, shape, dt, ctx)

            ii = s("ii", [P, P], I32)
            tri = s("tri", [P, P])
            ip = s("ip", [P, 1], I32)
            dsti = s("dsti", [B, EB], I32)
            srci = s("srci", [B, EB], I32)
            wrow = s("wrow", [B, EB])
            edge = {c: s(f"edge{c}", [B, EB]) for c in (0, 1, 3, 4)}
            edge[2] = wrow
            dstf = s("dstf", [B, EB])
            hii = s("hii", [B, EB], I32)
            prevl = s("prevl", [B, 1], I32)
            nextf = s("nextf", [B, 1], I32)
            pl = s("pl", [B, 2])
            start = s("start", [B, EB])
            pen = s("pen", [B, NB, P + 1])
            rowpen = s("rowpen", [B, 2, H, NB + 1])
            cum = s("cum", [B, EB])
            bf = s("bf", [B, NB])
            bi = s("bi", [B, NB], I32)
            ri = s("ri", [B, NB], I32)
            qi = s("qi", [B, NB // 4], I32)
            off = s("off", [B, 1])
            lrb = s("lrb", [B, EB], U8)
            meta = s("meta", [P, B, META, NB])
            zero = s("zero", [P, 1024])
            tp = [ctx.enter_context(nc.psum_tensor(f"tp{i}", [P, 4, P], F32)) for i in range(2)]
            offp = ctx.enter_context(nc.psum_tensor("offp", [P, 1], F32))
            sem = lambda n: ctx.enter_context(nc.semaphore(n))
            s_iota, s_pad, s_load, s_const = sem("s_iota"), sem("s_pad"), sem("s_load"), sem("s_const")
            s_cum, s_off, s_edge, s_tp, s_ev, s_st = (sem("s_cum"), sem("s_off"), sem("s_edge"), sem("s_tp"),
                                                      sem("s_ev"), sem("s_st"))
            block = ctx.enter_context(nc.Block())
            full = (B - 1) * EB

            @block.gpsimd
            def _(e):
                e.iota(ii[:, :], [[1, P]], base=0, channel_multiplier=0).then_inc(s_iota, 1)
                e.iota(ip[:, :], [[1, 1]], base=0, channel_multiplier=1).then_inc(s_iota, 1)

            @block.sync
            def _(e):
                e.wait_ge(s_pad, 1)
                for t, d in ((dsti, a["dst"]), (srci, a["src"]), (wrow, a["edge_weight"])):
                    e.dma_start(t[0:B - 1, :], d[0:full].rearrange("(b e) -> b e", e=EB)).then_inc(s_load, 16)
                    e.dma_start(t[B - 1:B, 0:ELAST], d[full:E].rearrange("(b e) -> b e", b=1)).then_inc(s_load, 16)
                d = a["dst"]
                e.dma_start(prevl[1:B, :], d[0:full].rearrange("(b e) -> b e", e=EB)[:, EB - 1:EB],
                            allow_slow_non_contiguous=True).then_inc(s_load, 16)
                e.dma_start(nextf[0:B - 2, :],
                            d[EB:full].rearrange("(b e) -> b e", e=EB)[:, 0:1],
                            allow_slow_non_contiguous=True).then_inc(s_load, 16)
                e.dma_start(nextf[B - 2:B - 1, :],
                            d[full:full + 1].rearrange("(b e) -> b e", b=1)).then_inc(s_load, 16)
                for k in range(DRANKS // P):
                    e.dma_start(bd_d[k * P:(k + 1) * P, :], zero[:, 0:F]).then_inc(s_st, 16)
                e.dma_start(sd_d.rearrange("(p k) h -> p (k h)", p=P),
                            zero[:, 0:DRANKS // P * 3 * H // 2].bitcast(BF16)).then_inc(s_st, 16)
                e.wait_ge(s_edge, 3)
                e.dma_start(base_d, bi[:, :]).then_inc(s_st, 16)
                e.dma_start(rel_d, ri[:, :]).then_inc(s_st, 16)
                e.dma_start(qbase_d, qi[:, :]).then_inc(s_st, 16)
                e.dma_start(wflat_d, wrow[:, :]).then_inc(s_st, 16)
                e.dma_start(pen_d, pen[:, :, :]).then_inc(s_st, 16)
                e.dma_start(rowpen_d.rearrange("b d k -> b (d k)"),
                            rowpen[:, :, :, :].rearrange("b d h k -> b (d h k)")).then_inc(s_st, 16)
                e.dma_start(lrrow_d, lrb[:, :]).then_inc(s_st, 16)
                e.wait_ge(s_ev, META * NB // 4)
                e.dma_start(meta_d.rearrange("b p c t -> p b (c t)"),
                            meta[:, :, :, :].rearrange("p b c t -> p b (c t)")).then_inc(s_st, 16)
                e.wait_ge(s_st, 16 * (DRANKS // P + 1 + 8))

            @block.vector
            def _(e):
                e.memset(zero[:, :], 0.0)
                e.memset(dsti[:, :], PAD_NODE)
                e.memset(srci[:, :], 0)
                e.memset(wrow[:, :], 0.0)
                e.memset(prevl[:, :], -1)
                e.memset(nextf[:, :], PAD_NODE)
                e.memset(ones[:, :], 1.0)
                e.drain().then_inc(s_pad, 1)
                e.wait_ge(s_iota, 2)
                e.tensor_copy(iota[:, :], ii[:, :])
                e.tensor_copy(iotab[:, :], ii[:, :])
                e.tensor_copy(iotap[:, :], ip[:, :])
                e.drain()
                one_hot(e, ident[:, :], iota[:, :], iotap[:, 0:1])
                e.tensor_scalar(tri[:, :], iota[:, :], iotap[:, 0:1], None, ALU.is_gt)
                e.drain().then_inc(s_const, 1)
                e.wait_ge(s_load, 16 * 9)
                e.tensor_copy(dstf[:, :], dsti[:, :])
                e.tensor_copy(edge[0][:, :], srci[:, :])
                e.tensor_scalar(hii[:, :], dsti[:, :], 7, None, ALU.arith_shift_right)
                e.tensor_copy(pl[:, 0:1], prevl[:, :])
                e.tensor_copy(pl[:, 1:2], nextf[:, :])
                e.drain()
                e.tensor_copy(edge[3][:, :], hii[:, :])
                e.tensor_tensor(start[:, 1:EB], dstf[:, 1:EB], dstf[:, 0:EB - 1], ALU.not_equal)
                e.tensor_tensor(start[:, 0:1], dstf[:, 0:1], pl[:, 0:1], ALU.not_equal)
                e.drain()
                e.scalar_tensor_tensor(edge[4][:, :], edge[3][:, :], -float(P), dstf[:, :], ALU.mult, ALU.add)
                e.tensor_tensor_scan(cum[:, :], start[:, :], start[:, :], 0.0, ALU.add, ALU.max)
                st = start[:, :].rearrange("b (t e) -> b t e", e=P)
                e.tensor_scalar(pen[:, :, 0:P], st, -BIG, None, ALU.mult)
                e.tensor_scalar(pen[:, 0:NB - 1, P:P + 1], st[:, 1:NB, 0:1], -BIG, None, ALU.mult)
                e.tensor_tensor(pl[:, 0:1], pl[:, 1:2], dstf[:, EB - 1:EB], ALU.not_equal)
                e.drain().then_inc(s_cum, 1)
                e.tensor_scalar(pen[:, NB - 1, P:P + 1], pl[:, 0:1], -BIG, None, ALU.mult)
                e.memset(rowpen[:, :, :, :], -BIG)
                ct = cum[:, :].rearrange("b (t e) -> b t e", e=P)
                e.tensor_tensor(edge[1][:, :].rearrange("b (t e) -> b t e", e=P), ct,
                                ct[:, :, 0:1].broadcast_to([B, NB, P]), ALU.subtract)
                e.drain()
                e.tensor_copy(lrb[:, :], edge[1][:, :])
                for h in range(H):
                    e.tensor_reduce(rowpen[:, 0, h, 1:NB + 1], pen[:, :, 0:P], AX.X, ALU.min)
                    e.tensor_reduce(rowpen[:, 1, h, 0:NB], pen[:, :, 1:P + 1], AX.X, ALU.min)
                e.wait_ge(s_off, 1)
                e.tensor_copy(off[:, :], offp[0:B, :])
                e.drain()
                e.tensor_scalar(bf[:, :], ct[:, :, 0], off[:, 0:1], -1.0, ALU.add, ALU.add)
                e.drain()
                e.tensor_copy(bi[:, :], bf[:, :])
                bq = bf[:, :].rearrange("b (q j) -> b q j", j=4)
                e.tensor_copy(qi[:, :], bq[:, :, 0])
                e.tensor_tensor(ri[:, :].rearrange("b (q j) -> b q j", j=4), bq,
                                bq[:, :, 0:1].broadcast_to([B, NB // 4, 4]), ALU.subtract)
                e.drain().then_inc(s_edge, 3)
                for k in range(META * NB // 4):
                    c, q = divmod(k, NB // 4)
                    e.wait_ge(s_tp, k + 1)
                    dstv = meta[:, :, c, 4 * q:4 * q + 4]
                    if c == 0:
                        dstv = meta[:, :, :, :].bitcast(I32)[:, :, c, 4 * q:4 * q + 4]
                    e.tensor_copy(dstv, tp[k % 2][:, :, 0:B].rearrange("p t b -> p b t")).then_inc(s_ev, 1)

            @block.tensor
            def _(e):
                e.wait_ge(s_cum, 1)
                e.wait_ge(s_const, 1)
                e.matmul(offp[0:B, :], tri[0:B, 0:B], cum[:, EB - 1:EB], start=True, stop=True).then_inc(s_off, 1)
                e.wait_ge(s_edge, 3)
                for k in range(META * NB // 4):
                    c, q = divmod(k, NB // 4)
                    if k >= 2:
                        e.wait_ge(s_ev, k - 1)
                    for j in range(4):
                        t = 4 * q + j
                        last = e.transpose(tp[k % 2][:, j, 0:B], edge[c][:, t * P:(t + 1) * P], ident[0:B, 0:B])
                    last.then_inc(s_tp, 1)

        with ExitStack() as ctx:
            xs = sb("xs", [P, NT, W0], F32, ctx)
            xw = sb("xw", [P, NT, F], F32, ctx)
            wb = sb("wb", [P, F], F32, ctx)
            s_z, s_x, s_sc, s_o = (ctx.enter_context(nc.semaphore(n)) for n in ("s_z", "s_x", "s_sc", "s_o"))
            block = ctx.enter_context(nc.Block())

            @block.sync
            def _(e):
                e.wait_ge(s_z, 1)
                e.dma_start(xs[:, 0:NT - 1, 0:F],
                            a["x"][0:(NT - 1) * P, :].rearrange("(t p) f -> p t f", p=P)).then_inc(s_x, 16)
                e.dma_start(xs[0:NLAST, NT - 1, 0:F], a["x"][(NT - 1) * P:N, :]).then_inc(s_x, 16)
                e.dma_start(wb[:, :], a["L0_gnn_W"][0:1, :].broadcast_to([P, F])).then_inc(s_x, 16)
                e.wait_ge(s_sc, 1)
                e.dma_start(t0_d.rearrange("(t p) f -> p t f", p=P), xs[:, :, :]).then_inc(s_o, 16)
                e.dma_start(x_d.rearrange("(t p) f -> p t f", p=P), xs[:, :, 0:F]).then_inc(s_o, 16)
                e.wait_ge(s_o, 32)

            @block.vector
            def _(e):
                e.memset(xs[:, NT - 1, :], 0.0)
                e.drain().then_inc(s_z, 1)
                e.wait_ge(s_x, 48)
                e.tensor_tensor(xw[:, :, :], xs[:, :, 0:F], wb[:, :].unsqueeze(1).broadcast_to([P, NT, F]), ALU.mult)
                e.drain()
                e.tensor_reduce(xs[:, :, F:F + 1], xw[:, :, :], AX.X, ALU.add)
                e.drain().then_inc(s_sc, 1)
        if stop <= 0:
            return

        consts = dict(iota=iota, iotab=iotab, iotap=iotap, ident=ident, ones=ones)
        d = dict(meta=meta_d, pen=pen_d, rowpen=rowpen_d, lrrow=lrrow_d, base=base_d, rel=rel_d, qbase=qbase_d,
                 wflat=wflat_d, rb=rb_d, deg=deg_d, x=x_d, t1=t1_d, t2=t2_d, t3=t3_d, sd=sd_d, bd=bd_d)

        with ExitStack() as ctx:
            acc = sb("acc0", [P, 1, RANKS], F32, ctx)
            den = sb("den0", [3, RANKS], F32, ctx)
            with nc.psum_tensor("hist", [NT, P], F32) as hist:
                edge_pass(nc, sb, "soft1", t0_d, W0, acc, den, hist, consts, d)
                if debug:
                    dump(nc, acc[:, :, :].rearrange("p a r -> p (a r)"), dram("acc0_d", (P, RANKS), F32))
                    dump(nc, den[:, :], dram("den0_d", (3, RANKS), F32))
                node_map(nc, sb, hist, consts, lrn, grank, dinv, rb_d, deg_d)
            if stop <= 1:
                return
            node_pass(nc, sb, 0, acc, den, lrn, grank, dinv, consts, a, d, out)
        if stop <= 2:
            return
        with ExitStack() as ctx:
            acc = sb("acc1", [P, 2, RANKS], F32, ctx)
            den = sb("den1", [3 * H, RANKS], F32, ctx)
            edge_pass(nc, sb, "soft4", t1_d, W1, acc, den, None, consts, dict(d, dst=sd_d))
            if debug:
                dump(nc, acc[:, :, :].rearrange("p a r -> p (a r)"), dram("acc1_d", (P, 2 * RANKS), F32))
                dump(nc, den[:, :], dram("den1_d", (3 * H, RANKS), F32))
            if stop <= 3:
                return
            node_pass(nc, sb, 1, acc, den, lrn, grank, dinv, consts, a, d, out)
        if stop <= 4:
            return
        with ExitStack() as ctx:
            acc = sb("acc2", [P, 1, RANKS], F32, ctx)
            edge_pass(nc, sb, "sum", t2_d, F, acc, None, None, consts, d)
            node_pass(nc, sb, 2, acc, None, lrn, grank, dinv, consts, a, d, out)
        if stop <= 5:
            return
        with ExitStack() as ctx:
            acc = sb("acc3", [P, 1, RANKS], F32, ctx)
            edge_pass(nc, sb, "mlp", t3_d, F, acc, None, None,
                      dict(consts, crow=a["L3_gnn_We1"][2 * F:2 * F + 1, :]), dict(d, dst=bd_d))
            node_pass(nc, sb, 3, acc, None, lrn, grank, dinv, consts, a, d, out)


def dump(nc, src, dst):
    with nc.semaphore("s_dump" + dst.tensor.name) as s, nc.Block() as block:
        @block.sync
        def _(e):
            e.dma_start(dst, src).then_inc(s, 16)
            e.wait_ge(s, 16)


class Batch:

    def __init__(self, U, off, it=0):
        self.b, self.par, self.turn = it * U + off, off % U, it + off // U


def batches(eng, U, body):
    body(None, Batch(U, 0))
    body(Batch(U, 0), Batch(U, 1))
    with eng.Fori(0, (B - 2) // U) as it:
        for i in range(U):
            body(Batch(U, 1 + i, it), Batch(U, 2 + i, it))
    body(Batch(U, B - 1), None)


def each_batch(eng, U, body):
    body(Batch(U, 0))
    body(Batch(U, 1))
    with eng.Fori(0, (B - 2) // U) as it:
        for i in range(U):
            body(Batch(U, 2 + i, it))


def load_values(nc, engine, ap, most):
    _, v = nc.values_load_multi_w_load_instructions(ap, engines=(engine,), min_val=0, max_val=most,
                                                    skip_runtime_bounds_check_because="no rank is above N")
    return v


def edge_pass(nc, sb, mode, table, width, acc, den, hist, c, d):
    soft = mode in ("soft1", "soft4")
    heads = H if mode == "soft4" else 1
    dst_w = {"soft4": 3 * H, "mlp": F}.get(mode, 0)
    R = heads * NB
    K1 = NB + 1
    blocks = 2 if mode == "soft4" else 1
    n_ld = 1 + (heads + 1 if soft else 0) + (1 + NB if dst_w else 0) + (mode == "mlp")
    NQ = NB // 4
    U = 2 if mode == "soft4" else 3
    NS = 2 if mode == "soft4" else 4
    NLRB = 1 if soft else U
    PE, DVE, SP = mybir.EngineType.PE, mybir.EngineType.DVE, mybir.EngineType.SP
    iota, ident, ones = c["iota"], c["ident"], c["ones"]
    with ExitStack() as ctx:
        def s(name, shape, dt=F32):
            return sb(f"{name}_{mode}", shape, dt, ctx)

        def ps(name, shape):
            return ctx.enter_context(nc.psum_tensor(f"{name}_{mode}", shape, F32))

        def sem(name):
            return ctx.enter_context(nc.semaphore(f"{name}_{mode}"))

        rows = s("rows", [P, U, NB, width])
        idx = s("idx", [P, U, NB])
        mt = s("mt", [P, U, META - 1, NB])
        S = s("S", [P, NS, 4, P])
        zb = s("zb", [P, 512], BF16)
        if soft:
            Sb = s("Sb", [P, NS, 4, P], BF16)
            pen = s("pen", [R, U, P + 1])
            rowpen = s("rowpen", [1, U, 2, heads * K1])
            sc = s("sc", [P, heads, NB])
            f1, f2, b1 = (s(n, [R, P]) for n in ("f1", "f2", "b1"))
            m, wr = f1, b1
            col = s("col", [R, 2])
            R_, I_, RB_, J_ = (s(n, [1, heads, K1]) for n in ("Rr", "Ir", "RBr", "Jr"))
            al = s("al", [1, heads])
            if heads > 1:
                line = s("line", [1, R])
            alpha = s("alpha", [P, U, blocks])
            alphad = s("alphad", [3 * heads, U])
            al3 = s("al3", [1, 3, heads])
            wc = s("wc", [P, U, heads, NB])
            rest = s("rest", [P, heads, NB])
            w3 = s("w3", [P, U, NB, 3, heads], BF16)
            scT = ps("scT", [R, P])
            small = ps("small", [P, 512])
            rp1, rp2, cp1, cp2 = small[0:1, 0:R], small[0:1, 64:64 + R], small[0:R, 128:129], small[0:R, 132:133]
            ap, adp = small[:, 136:136 + blocks], small[0:3 * heads, 140:141]
            ex, wp = small[:, 192:192 + R], small[:, 256:256 + R]
            pd = [ps(f"pd{i}", [3 * heads, 512]) for i in range(2)]
        if mode == "soft1":
            ho = s("ho", [P, NS, 4, NT], BF16)
            lo = s("lo", [P, NS, 4, P], BF16)
        if dst_w:
            lrb = s("lrb", [P, NLRB, EB], U8)
            dw = s("dw", [P, U, NB, dst_w], BF16 if soft else F32)
            ST = s("ST", [P, 2, 4, P], BF16 if soft else F32)
        if mode == "mlp":
            wrow = s("wrow", [1, U, EB])
            crow = s("crow", [1, F])
            pre = [ps(f"pre{i}", [P, 4, P]) for i in range(2)]
        pn = [[ps(f"pn{i}{k}", [P, 512]) for k in range(blocks)] for i in range(2)]
        s_ld = [sem(f"s_ld{i}") for i in range(U)]
        s_md = [sem(f"s_md{i}") for i in range(U)]
        s_g = [sem(f"s_g{i}") for i in range(U)]
        s_rs = sem("s_rs")
        s_k = sem("s_k")
        s_mm, s_add, s_S, s_Sb = sem("s_mm"), sem("s_add"), sem("s_S"), sem("s_Sb")
        s_A, s_st, s_ex, s_pre, s_init, s_c = (sem("s_A"), sem("s_st"), sem("s_ex"), sem("s_pre"),
                                               sem("s_init"), sem("s_c"))
        block = ctx.enter_context(nc.Block())

        def a_score(e, bt):
            e.wait_ge(s_g[bt.par], (bt.turn + 1) * (16 * NB))
            g = rows[:, bt.par, :, width - heads:width].rearrange("p t h -> p h t")
            if heads == 1:
                return e.tensor_copy(sc[:, :, :], g)
            e.wait_ge(s_ex, bt.b * NQ + NQ)
            e.tensor_tensor(sc[:, :, :], g, ex.rearrange("p (t h) -> p h t", h=heads), ALU.add)
            e.drain()
            return e.scalar_tensor_tensor(sc[:, :, :], sc[:, :, :], 0.2, sc[:, :, :], ALU.mult, ALU.max)

        def a_scoreT(e, bt):
            return e.transpose(scT[:, :], sc[:, :, :].rearrange("p h t -> p (h t)"), ident[:, :])

        def a_scan1(e, bt):
            e.wait_ge(s_ld[bt.par], (bt.turn + 1) * (16 * n_ld))
            return e.tensor_tensor_scan(f1[:, :], pen[:, bt.par, 0:P], scT[:, :], -BIG, ALU.add, ALU.max)

        def a_rowF(e, bt):
            return e.transpose(rp1, f1[:, P - 1:P], ident[0:R, 0:R])

        def a_scanI(e, bt):
            e.tensor_copy(R_[:, :, 0:1], I_[:, :, NB:K1])
            e.tensor_copy(R_[:, :, 1:K1], rp1.rearrange("o (h t) -> o h t", h=heads))
            e.drain()
            last = e.tensor_tensor_scan(I_[:, :, :].rearrange("o h k -> o (h k)"), rowpen[:, bt.par, 0, :],
                                        R_[:, :, :].rearrange("o h k -> o (h k)"), -BIG, ALU.add, ALU.max)
            return reach(e, last, I_[:, :, 0:NB])

        def reach(e, last, entries):
            if heads == 1:
                return last
            e.drain()
            return e.tensor_copy(line[:, :].rearrange("o (h t) -> o h t", h=heads), entries)

        def a_colI(e, bt):
            return e.transpose(cp1, I_[:, 0, 0:NB] if heads == 1 else line[:, :], ident[0:1, 0:1])

        def a_scan2(e, bt):
            e.tensor_copy(col[:, 0:1], cp1)
            e.drain()
            e.tensor_tensor_scan(f2[:, :], pen[:, bt.par, 0:P], scT[:, :], col[:, 0:1], ALU.add, ALU.max)
            e.drain()
            return e.tensor_tensor_scan(b1[:, ::-1], pen[:, bt.par, P:0:-1], f2[:, ::-1], -BIG, ALU.add, ALU.max)

        def a_rowB(e, bt):
            return e.transpose(rp2, b1[:, 0:1], ident[0:R, 0:R])

        def a_scanJ(e, bt):
            e.tensor_copy(RB_[:, :, 0:NB], rp2.rearrange("o (h t) -> o h t", h=heads))
            e.drain()
            e.tensor_tensor_scan(J_[:, :, :].rearrange("o h k -> o (h k)")[:, ::-1], rowpen[:, bt.par, 1, ::-1],
                                 RB_[:, :, :].rearrange("o h k -> o (h k)")[:, ::-1], -BIG, ALU.add, ALU.max)
            e.drain()
            e.tensor_tensor(al[:, :], R_[:, :, 0], J_[:, :, 0], ALU.subtract)
            e.drain()
            if heads > 1:
                reach(e, None, J_[:, :, 1:K1])
            return e.tensor_scalar(al3[:, :, :], al[:, :].unsqueeze(1).broadcast_to([1, 3, heads]), 0.0, None, ALU.min)

        def a_colJ(e, bt):
            return e.transpose(cp2, J_[:, 0, 1:K1] if heads == 1 else line[:, :], ident[0:1, 0:1])

        def a_alpha(e, bt):
            return e.activation(al3[:, :, :], al3[:, :, :], ACT.Exp)

        def a_alphab(e, bt):
            if heads == 1:
                e.matmul(ap, ones[0:1, :], al3[:, 0, :], start=True, stop=True)
            else:
                for i in range(2):
                    e.matmul(ap[i * DH:(i + 1) * DH, :], ones[0:1, 0:DH], al3[:, 0, i:heads:2], start=True, stop=True)
            return e.transpose(adp, al3[:, :, :].rearrange("o k h -> o (k h)"), ident[0:1, 0:1])

        def a_scan3(e, bt):
            e.tensor_copy(col[:, 1:2], cp2)
            e.tensor_copy(alpha[:, bt.par, :], ap)
            e.tensor_copy(alphad[:, bt.par:bt.par + 1], adp)
            e.drain()
            e.tensor_tensor_scan(m[:, ::-1], pen[:, bt.par, P:0:-1], f2[:, ::-1], col[:, 1:2], ALU.add, ALU.max)
            e.drain()
            return e.tensor_tensor(wr[:, :], scT[:, :], m[:, :], ALU.subtract)

        def a_exp(e, bt):
            return e.activation(wr[:, :], wr[:, :], ACT.Exp)

        def a_wT(e, bt):
            return e.transpose(wp, wr[:, :], ident[0:R, 0:R])

        def a_wc(e, bt):
            return e.copy(wc[:, bt.par, :, :], wp.rearrange("p (h t) -> p h t", h=heads))

        def a_split(e, bt):
            w = wc[:, bt.par, :, :]
            part = [w3[:, bt.par, :, k, :].rearrange("p t h -> p h t") for k in range(3)]
            e.tensor_copy(part[0], w)
            e.drain()
            e.tensor_tensor(rest[:, :, :], w, part[0], ALU.subtract)
            e.drain()
            e.tensor_copy(part[1], rest[:, :, :])
            e.drain()
            return e.tensor_tensor(part[2], rest[:, :, :], part[1], ALU.subtract)

        stages = [("dve", 4, a_score), ("pe", 4, a_scoreT), ("dve", 5, a_scan1), ("pe", 5, a_rowF),
                  ("dve", 6, a_scanI), ("pe", 6, a_colI), ("dve", 8, a_scan2), ("pe", 8, a_rowB),
                  ("dve", 9, a_scanJ), ("pe", 9, a_colJ), ("act", 9, a_alpha), ("pe", 10, a_alphab),
                  ("dve", 12, a_scan3), ("act", 12, a_exp), ("pe", 13, a_wT), ("act", 13, a_wc),
                  ("dve", 15, a_split)]
        NA = {"soft1": len(stages), "soft4": len(stages), "sum": 1, "mlp": NQ}[mode]

        def prepare(e, who, slot, bt):
            for k, (w, sl, fn) in enumerate(stages if soft else []):
                if w == who and sl == slot:
                    e.wait_ge(s_A, (bt.b + U) * NA + k)
                    if who == "pe":
                        e.sem_inc(s_k, 1)
                    fn(e, bt).then_inc(s_A, 1)

        @block.sync
        def _(e):
            if mode == "mlp":
                e.dma_start(crow[:, :], c["crow"]).then_inc(s_c, 16)

            def body(bt):
                e.wait_ge(s_A, (bt.b + 1) * NA)
                e.sem_inc(s_k, 1)
                ld = s_ld[bt.par]
                e.dma_start(idx[:, bt.par, :], d["meta"][bass.ds(bt.b, 1), :, 0, :].rearrange("o p t -> (o p) t")).then_inc(ld, 16)
                if soft:
                    for h in range(heads):
                        e.dma_start(pen[h * NB:(h + 1) * NB, bt.par, :],
                                    d["pen"][bass.ds(bt.b, 1), :, :].rearrange("o t e -> (o t) e")).then_inc(ld, 16)
                    e.dma_start(rowpen[:, bt.par, :, :],
                                d["rowpen"][bass.ds(bt.b, 1), :, 0:heads * K1]).then_inc(ld, 16)
                if mode == "mlp":
                    e.dma_start(wrow[:, bt.par, :], d["wflat"][bass.ds(bt.b, 1), :]).then_inc(ld, 16)
                if dst_w:
                    for q in range(NQ):
                        r0 = load_values(nc, SP, d["base"][bass.ds(bt.b, 1), q * 4:q * 4 + 4], N)
                        for j in range(4):
                            e.dma_start(dw[:, bt.par, q * 4 + j, :], d["dst"][bass.ds(r0[j], P), :]).then_inc(ld, 16)
                    if NLRB == 1:
                        e.wait_ge(s_st, bt.b * NQ + NQ)
                        e.sem_inc(s_k, 1)
                    e.dma_start(lrb[:, bt.par % NLRB, :], d["lrrow"][bass.ds(bt.b, 1), :].broadcast_to([P, EB])).then_inc(ld, 16)
            each_batch(e, U, body)

        @block.gpsimd
        def _(e):
            def body(bt):
                for j in range(NB):
                    if j == 0:
                        e.wait_ge(s_ld[bt.par], (bt.turn + 1) * (16 * n_ld))
                        e.sem_inc(s_k, 1)
                    if j % 4 == 0:
                        e.wait_ge(s_mm, bt.b * NQ + j // 4 + 1)
                        e.sem_inc(s_k, 1)
                    e.indirect_dma_start(rows[:, bt.par, j, :], None, table,
                                         bass.IndirectOffsetOnAxis(ap=idx[:, bt.par, j:j + 1].bitcast(I32), axis=0)
                                         ).then_inc(s_g[bt.par], 16)
            each_batch(e, U, body)

        @block.scalar
        def _(e):
            def scale(bs, q):
                for j in ACT_TILES[mode]:
                    t = 4 * q + j
                    for h in range(heads):
                        wid = F if heads == 1 else DH
                        g = rows[:, bs.par, t, h * wid:(h + 1) * wid]
                        e.activation(g, g, ACT.Copy, scale=wc[:, bs.par, h, t:t + 1])
                e.wait_ge(s_S, bs.b * NQ + q + 1)
                e.copy(Sb[:, q % NS, :, :], S[:, q % NS, :, :]).then_inc(s_Sb, 1)

            def body(bs, bp):
                if bs is not None and soft:
                    e.wait_ge(s_A, (bs.b + U + 1) * NA)
                    scale(bs, 0)
                if bp is not None:
                    e.wait_ge(s_mm, bp.b * NQ + NQ)
                    e.sem_inc(s_k, 1)
                    e.dma_start(mt[:, bp.par, :, :],
                                d["meta"][bass.ds(bp.b, 1), :, 1:META, :].rearrange("o p c t -> (o p) c t")
                                ).then_inc(s_md[bp.par], 16)
                for k in range(NB):
                    if bs is not None and soft and k % 4 == 1 and k // 4 + 1 < NQ:
                        scale(bs, k // 4 + 1)
                    if bp is not None:
                        prepare(e, "act", k, bp)
                        if mode == "mlp" and k % 4 == 2:
                            q = k // 4
                            e.wait_ge(s_pre, bp.b * NQ + q + 3)
                            g = rows[:, bp.par, 4 * q:4 * q + 4, :]
                            e.activation(g, g, ACT.Gelu).then_inc(s_A, 1)
            batches(e, U, body)

        @block.tensor
        def _(e):
            e.sem_inc(s_mm, U * NQ)
            e.wait_ge(s_init, 1)
            if mode == "soft1":
                e.matmul(hist[:, :], zb[:, 0:NT], zb[:, 0:P], start=True, stop=False)
            if mode == "mlp":
                e.wait_ge(s_c, 16)

            def first_ranks(bs, q):
                return load_values(nc, PE, d["rel"][bass.ds(bs.b, 1), 4 * q:4 * q + 4], 3 * P)

            def body(bs, bp):
                if bs is not None:
                    nxt = first_ranks(bs, 0)
                for k in range(NB):
                    q, j = divmod(k, 4)
                    if bp is not None:
                        if dst_w and (k < NQ if soft else j == 0):
                            qq = k if soft else q
                            if soft and qq == 0:
                                e.wait_ge(s_A, (bp.b + U) * NA)
                            if not soft:
                                e.wait_ge(s_pre, bp.b * NQ + qq + 1)
                            e.wait_ge(s_st, bp.b * NQ + qq + 1 + (NQ if NLRB == 1 else 0))
                            e.sem_inc(s_k, 1)
                            for i in range(4):
                                t = 4 * qq + i
                                if soft:
                                    for part in range(3):
                                        last = e.matmul(ex[:, t * heads:(t + 1) * heads], ST[:, qq % 2, i, :],
                                                        dw[:, bp.par, t, part * heads:(part + 1) * heads],
                                                        start=(part == 0), stop=(part == 2))
                                else:
                                    e.matmul(pre[qq % 2][:, i, :], ST[:, qq % 2, i, :], dw[:, bp.par, t, :],
                                             start=True, stop=False)
                                    last = e.matmul(pre[qq % 2][:, i, :], wrow[:, bp.par, t * P:(t + 1) * P],
                                                    crow[:, :], start=False, stop=True)
                            last.then_inc(s_ex, 1)
                        prepare(e, "pe", k, bp)
                    if bs is not None:
                        n = bs.b * NQ + q
                        if j == 0:
                            rel = nxt
                            e.wait_ge(s_Sb if soft else s_S, n + 1)
                            if mode == "soft4":
                                e.wait_ge(s_rs, n + 1)
                            if mode == "mlp":
                                e.wait_ge(s_A, (bs.b + U) * NA + q + 1)
                            e.wait_ge(s_add, n + 1)
                            e.sem_inc(s_k, 1)
                            banks = [x[:, :] for x in pn[q % 2]]
                            for x in banks:
                                e.matmul(x, zb[:, 0:P], zb[:, :], start=True, stop=False)
                            if soft:
                                e.matmul(pd[q % 2][:, :], zb[:, 0:3 * heads], zb[:, :], start=True, stop=False)
                        w = bass.ds(rel[j], P)
                        for i in range(blocks):
                            last = e.matmul(pn[q % 2][i][:, w], rows[:, bs.par, k, i * P:(i + 1) * P],
                                            S[:, q % NS, j, :], start=False, stop=(j == 3))
                        if soft:
                            last = e.matmul(pd[q % 2][:, w], w3[:, bs.par, k, :, :].rearrange("p k h -> p (k h)"),
                                            Sb[:, q % NS, j, :], start=False, stop=(j == 3))
                        if mode == "soft1":
                            last = e.matmul(hist[:, :], ho[:, q % NS, j, :], lo[:, q % NS, j, :], start=False, stop=False)
                        if j == 1 and q + 1 < NQ:
                            nxt = first_ranks(bs, q + 1)
                        if j == 3:
                            last.then_inc(s_mm, 1)
            batches(e, U, body)
            if mode == "soft1":
                e.matmul(hist[:, :], zb[:, 0:NT], zb[:, 0:P], start=False, stop=True)

        @block.vector
        def _(e):
            qbase = d["qbase"].rearrange("(o b) q -> o (b q)", o=1)
            e.memset(acc[:, :, :], 0.0)
            e.memset(zb[:, :], 0.0)
            if soft:
                e.memset(den[:, :], 0.0)
                e.memset(I_[:, :, :], -BIG)
                e.memset(RB_[:, :, :], -BIG)
            e.drain().then_inc(s_init, 1)
            e.sem_inc(s_A, U * NA)
            e.sem_inc(s_add, 2)
            if mode == "mlp":
                e.sem_inc(s_pre, 2)
            if dst_w and NLRB == 1:
                e.sem_inc(s_st, NQ)

            def make1(bt, q):
                if q == 0:
                    e.wait_ge(s_md[bt.par], (bt.turn + 1) * 16)
                e.wait_ge(s_mm, bt.b * NQ + (q + U * NQ + 1 - NS))
                if mode == "soft1":
                    sl = slice(4 * q, 4 * q + 4)
                    e.tensor_tensor(ho[:, q % NS, :, :], c["iotab"][:, 0:NT].unsqueeze(1).broadcast_to([P, 4, NT]),
                                    mt[:, bt.par, 2, sl].unsqueeze(2).broadcast_to([P, 4, NT]), ALU.is_equal)

            def make2(bt, q):
                sl = slice(4 * q, 4 * q + 4)
                if mode == "soft1":
                    e.tensor_tensor(lo[:, q % NS, :, :], c["iotab"][:, :].unsqueeze(1).broadcast_to([P, 4, P]),
                                    mt[:, bt.par, 3, sl].unsqueeze(2).broadcast_to([P, 4, P]), ALU.is_equal)
                e.tensor_tensor(S[:, q % NS, :, :], iota[:, :].unsqueeze(1).broadcast_to([P, 4, P]),
                                mt[:, bt.par, 0, sl].unsqueeze(2).broadcast_to([P, 4, P]), ALU.is_equal).then_inc(s_S, 1)

            def scale(bs, q):
                n = 4 - len(ACT_TILES[mode])
                g = rows[:, bs.par, 4 * q:4 * q + n, 0:H * DH].rearrange("p t (h d) -> p t h d", h=H)
                w = wc[:, bs.par, :, 4 * q:4 * q + n].rearrange("p h t -> p t h").unsqueeze(3)
                e.tensor_tensor(g, g, w.broadcast_to([P, n, H, DH]), ALU.mult).then_inc(s_rs, 1)

            def add(n, q, r0):
                e.drain()
                e.wait_ge(s_mm, n + (U * NQ + 1))
                for i in range(blocks):
                    w = acc[:, i, bass.ds(r0, 4 * P)]
                    last = e.tensor_tensor(w, w, pn[q % 2][i][:, :], ALU.add)
                if soft:
                    w = den[:, bass.ds(r0, 4 * P)]
                    last = e.tensor_tensor(w, w, pd[q % 2][:, :], ALU.add)
                last.then_inc(s_add, 1)

            def rescale(bs, r0):
                e.drain()
                first = acc[:, :, bass.ds(r0, 1)]
                e.tensor_tensor(first, first, alpha[:, bs.par, :].unsqueeze(2), ALU.mult)
                fd = den[:, bass.ds(r0, 1)]
                e.tensor_tensor(fd, fd, alphad[:, bs.par:bs.par + 1], ALU.mult)

            def body(bs, bp):
                if bs is not None:
                    n = bs.b * NQ
                    if isinstance(bs.b, int) and bs.b == 0:
                        before, r0 = None, load_values(nc, DVE, qbase[:, 0:NQ], N)
                    else:
                        before, *r0 = load_values(nc, DVE, qbase[:, bass.ds(n - 1, NQ + 1)], N)
                    if soft:
                        e.wait_ge(s_A, (bs.b + U + 1) * NA)
                    if mode == "soft4":
                        scale(bs, 0)
                for k in range(NB):
                    q, j = divmod(k, 4)
                    bt, nq = (bs, q + 1) if q + 1 < NQ else (bp, 0)
                    if bt is not None and j == 0:
                        make1(bt, nq)
                    if bt is not None and j == 1:
                        make2(bt, nq)
                    if mode == "soft4" and bs is not None and j == 2 and q + 1 < NQ:
                        scale(bs, q + 1)
                    if bp is not None:
                        if dst_w and (k < NQ if soft else j == 0):
                            for qq in (k if soft else q,):
                                if qq == 0:
                                    e.wait_ge(s_ld[bp.par], (bp.turn + 1) * (16 * n_ld))
                                if qq >= 2:
                                    e.wait_ge(s_ex, bp.b * NQ + qq - 1)
                                one_hot(e, ST[:, qq % 2, :, :].rearrange("p t e -> p (t e)"),
                                        lrb[:, bp.par % NLRB, qq * 4 * P:(qq + 1) * 4 * P],
                                        c["iotap"][:, 0:1]).then_inc(s_st, 1)
                        if mode == "mlp" and j == 1:
                            if q == 0:
                                e.wait_ge(s_g[bp.par], (bp.turn + 1) * (16 * NB))
                            e.wait_ge(s_ex, bp.b * NQ + q + 1)
                            g = rows[:, bp.par, 4 * q:4 * q + 4, :]
                            e.tensor_tensor(g, g, pre[q % 2][:, :, :], ALU.add).then_inc(s_pre, 1)
                        if mode == "sum" and k == 0:
                            e.wait_ge(s_g[bp.par], (bp.turn + 1) * (16 * NB))
                            e.sem_inc(s_A, 1)
                        prepare(e, "dve", k, bp)
                    if bs is not None and j == 1:
                        if q > 0:
                            if soft and q == 1:
                                rescale(bs, r0[0])
                            add(n + (q - 1), q - 1, r0[q - 1])
                        elif before is not None:
                            add(n - 1, NQ - 1, before)
                if bp is None:
                    add(n + (NQ - 1), NQ - 1, r0[NQ - 1])
            batches(e, U, body)


ACT_TILES = {"soft1": (0, 1, 2, 3), "soft4": (3,), "sum": (), "mlp": ()}


def node_map(nc, sb, hist, c, lrn, grank, dinv, rb_d, deg_d):
    with ExitStack() as ctx:
        d, ne, cum, lr, lrm, gr, gm = (sb(f"nm_{n}", [NT, P], F32, ctx)
                                       for n in ("d", "ne", "cum", "lr", "lrm", "gr", "gm"))
        rb, rbi = sb("nm_rb", [NT, 1], F32, ctx), sb("nm_rbi", [NT, 1], I32, ctx)
        off = ctx.enter_context(nc.psum_tensor("nm_off", [P, 512], F32))
        tp = ctx.enter_context(nc.psum_tensor("nm_tp", [P, 3, P], F32))
        dc = sb("nm_dc", [P, NT], F32, ctx)
        s_c, s_o, s_r, s_t, s_d, s_v = (ctx.enter_context(nc.semaphore(f"nm_{n}")) for n in "cortdv")
        s_q = ctx.enter_context(nc.semaphore("nm_q"))
        tri = sb("nm_tri", [P, P], F32, ctx)
        block = ctx.enter_context(nc.Block())

        @block.vector
        def _(e):
            e.tensor_copy(d[:, :], hist[:, :])
            e.tensor_scalar(tri[:, :], c["iota"][:, :], c["iotap"][:, 0:1], None, ALU.is_gt)
            e.drain()
            e.tensor_scalar(ne[:, :], d[:, :], 1.0, None, ALU.min)
            e.drain()
            e.tensor_tensor_scan(cum[:, :], ne[:, :], ne[:, :], 0.0, ALU.add, ALU.max)
            e.drain().then_inc(s_c, 1)
            e.tensor_tensor(lr[:, :], cum[:, :], ne[:, :], ALU.mult)
            e.drain()
            e.tensor_scalar(lrm[:, :], lr[:, :], -1.0, None, ALU.add)
            e.wait_ge(s_o, 1)
            e.tensor_copy(rbi[:, :], off[0:NT, 0:1])
            e.tensor_copy(rb[:, :], off[0:NT, 0:1])
            e.tensor_scalar(gm[:, :], ne[:, :], -float(1 << 20), float(1 << 20), ALU.mult, ALU.add)
            e.drain()
            e.scalar_tensor_tensor(gr[:, :], lrm[:, :], rb[:, 0:1], gm[:, :], ALU.add, ALU.add)
            e.drain().then_inc(s_r, 1)
            e.wait_ge(s_t, 1)
            e.tensor_copy(lrn[:, :], tp[:, 0, 0:NT])
            e.tensor_scalar(dc[:, :], tp[:, 1, 0:NT], 1.0, None, ALU.add)
            e.tensor_copy(grank[:, :], tp[:, 2, 0:NT])
            e.drain().then_inc(s_v, 1)
            e.wait_ge(s_q, 1)
            e.reciprocal(dinv[:, :], dc[:, :])

        @block.scalar
        def _(e):
            e.wait_ge(s_v, 1)
            e.activation(dc[:, :], dc[:, :], ACT.Sqrt).then_inc(s_q, 1)

        @block.tensor
        def _(e):
            e.wait_ge(s_c, 1)
            e.matmul(off[0:NT, 0:1], tri[0:NT, 0:NT], cum[:, P - 1:P], start=True, stop=True).then_inc(s_o, 1)
            e.wait_ge(s_r, 1)
            for i, t in enumerate((lrm, d, gr)):
                last = e.transpose(tp[:, i, 0:NT], t[:, :], c["ident"][0:NT, 0:NT])
            last.then_inc(s_t, 1)

        @block.sync
        def _(e):
            e.wait_ge(s_r, 1)
            e.dma_start(rb_d, rbi[:, :]).then_inc(s_d, 16)
            e.dma_start(deg_d, d[:, :]).then_inc(s_d, 16)
            e.wait_ge(s_d, 32)


def node_pass(nc, sb, layer, acc, den, lrn, grank, dinv, c, a, d, out):
    nchain = 1 if layer == 1 else 2
    blocks, parts, heads = {0: (1, 3, 1), 1: (2, 3 * H, H), 2: (1, 0, 1), 3: (1, 0, 1)}[layer]
    K = blocks * F
    PE, DVE, SP = mybir.EngineType.PE, mybir.EngineType.DVE, mybir.EngineType.SP
    ident, iota = c["ident"], c["iota"]
    with ExitStack() as ctx:
        def s(name, shape, dt=F32):
            return sb(f"n{layer}_{name}", shape, dt, ctx)

        def ps(name, shape):
            return ctx.enter_context(nc.psum_tensor(f"n{layer}_{name}", shape, F32))

        def sem(name):
            return ctx.enter_context(nc.semaphore(f"n{layer}_{name}"))

        s_held, s_w, s_p, s_p2, s_z = sem("s_held"), sem("s_w"), sem("s_p"), sem("s_p2"), sem("s_z")
        loads, prep = [], []

        def weight(name, shape, ap):
            t = s(name, shape)
            loads.append((t, ap))
            return t

        if layer == 0:
            wn = weight("wn", [P, H, DH], a["L1_gnn_W_n"].rearrange("h c d -> c h d"))
            wnT = weight("wnT", [DH, H, F], a["WnT"])
            a2 = weight("a2", [DH, 2, H], a["aT"])
            vs = s("vs", [P, 2, H])
            vps = []
        if layer == 1:
            w1 = weight("w1", [P, 2, 2 * F], a["L1_gnn_mlp_W1"].rearrange("(k p) j -> p k j", p=P))
            w2 = weight("w2", [P, 2, F], a["L1_gnn_mlp_W2"].rearrange("(k p) j -> p k j", p=P))
            b1 = weight("b1", [P, 2], a["L1_gnn_mlp_b1"].rearrange("(k p) -> p k", p=P))
            b2 = weight("b2", [P, F], a["L1_gnn_mlp_b2"].rearrange("(o f) -> o f", o=1).broadcast_to([P, F]))
            wg = weight("wg", [P, F], a["L2_gnn_W"])
        if layer == 2:
            b2 = weight("b2", [P, F], a["L2_gnn_b"].rearrange("(o f) -> o f", o=1).broadcast_to([P, F]))
            we = weight("we", [P, 2, F], a["L3_gnn_We1"][0:2 * F, :].rearrange("(k p) j -> p k j", p=P))
            be = weight("be", [P, F], a["L3_gnn_be1"].rearrange("(o f) -> o f", o=1).broadcast_to([P, F]))
        if layer == 3:
            row = lambda n: a[n].rearrange("(o f) -> o f", o=1)
            we2 = weight("we2", [P, F], a["L3_gnn_We2"])
            be2 = weight("be2", [1, F], row("L3_gnn_be2"))
            wu = weight("wu", [P, 2, F], a["L3_gnn_Wu1"].rearrange("(k p) j -> p k j", p=P))
            bu = weight("bu", [P, 1], a["L3_gnn_bu1"].rearrange("(p o) -> p o", o=1))
            wu2 = weight("wu2", [P, F], a["L3_gnn_Wu2"])
            b2 = weight("b2", [P, F], row("L3_gnn_bu2").broadcast_to([P, F]))
            gam = weight("gam", [P, F], row("L3_gnn_gamma").broadcast_to([P, F]))
            bet = weight("bet", [P, F], row("L3_gnn_beta").broadcast_to([P, F]))

        x_t = d["x"].rearrange("(g t p) f -> g p t f", t=G, p=P)
        GF = [P, G, F]

        def make_chain(ci):
            n = lambda name, shape, dt=F32: s(f"{name}{ci}", shape, dt)
            sm = sem(f"s_c{ci}")
            s_scat = sem(f"s_scat{ci}")
            x, y = n("x", GF), n("y", GF)
            ET, Es = n("ET", GF), n("Es", GF)
            win = n("win", [P, blocks, G, F])
            Ar = n("Ar", [P, G, K])
            st6, mv = n("st6", [P, G, 6]), n("mv", [P, G, 2])
            rs = n("rs", [P, G, 1])
            pE = ps(f"pE{ci}", [P, 8, P])
            pA = ps(f"pA{ci}", [P, blocks, 8, P])
            if layer == 0:
                vps.append(pE[:, 7, 0:2 * H])
            if parts:
                dwin = n("dwin", [parts, G, P])
                dd, rd = n("dd", [P, G, heads]), n("rd", [P, G, heads])
                pD = pE[:, 7, 0:G * parts].rearrange("p (t k) -> p t k", k=parts)
            stages = []
            S_ = lambda who, w=1: (lambda fn: stages.append((who, w, fn)) or fn)

            @S_("sp", 16)
            def _(e, sem):
                e.dma_start(x[:, :, :], x_t[bass.ds(cur["g"], 1)].rearrange("o p t f -> (o p) t f")).then_inc(sem, 16)

            @S_("dve")
            def _(e, sem):
                rb = load_values(nc, DVE, d["rb"].rearrange("(g t) o -> g (o t)", t=G)[bass.ds(cur["g"], 1), :], N)
                e.tensor_tensor(ET[:, :, :], iota[:, :].unsqueeze(1).broadcast_to(GF),
                                lrn[:, bass.ds(cur["g"] * G, G)].unsqueeze(2).broadcast_to(GF), ALU.is_equal)
                for t in range(G):
                    last = e.tensor_copy(win[:, :, t, :], acc[:, :, bass.ds(rb[t], P)])
                    if parts:
                        last = e.tensor_copy(dwin[:, t, :], den[:, bass.ds(rb[t], P)])
                last.then_inc(sem, 1)

            @S_("pe")
            def _(e, sem):
                for t in range(G):
                    last = e.transpose(pE[:, t, :], ET[:, t, :], ident[:, :])
                    for k in range(blocks):
                        last = e.transpose(pA[:, k, t, :], win[:, k, t, :], ident[:, :])
                    if parts:
                        last = e.transpose(pD[:, t, :], dwin[:, t, :], ident[0:parts, 0:parts])
                last.then_inc(sem, 1)

            @S_("dve")
            def _(e, sem):
                last = e.tensor_copy(Es[:, :, :], pE[:, 0:G, :])
                if parts:
                    e.tensor_reduce(dd[:, :, :], pD.rearrange("p t (k h) -> p t h k", k=3), AX.X, ALU.add)
                    e.drain()
                    e.tensor_scalar(dd[:, :, :], dd[:, :, :], 1e-20, None, ALU.max)
                    e.drain()
                    e.reciprocal(rd[:, :, :], dd[:, :, :])
                    e.drain()
                for k in range(blocks):
                    o = Ar[:, :, k * F:(k + 1) * F]
                    if not parts:
                        last = e.tensor_copy(o, pA[:, k, 0:G, :])
                    elif heads == 1:
                        last = e.tensor_tensor(o, pA[:, k, 0:G, :], rd[:, :, :].broadcast_to(GF), ALU.mult)
                    else:
                        for h in range(2):
                            hs = slice(h * DH, (h + 1) * DH)
                            last = e.tensor_tensor(o[:, :, hs], pA[:, k, 0:G, hs],
                                                   rd[:, :, 2 * k + h:2 * k + h + 1].broadcast_to([P, G, DH]), ALU.mult)
                last.then_inc(sem, 1)

            def layernorm(e, src, dst, dst_scale=None):
                for t in range(G):
                    e.bn_stats(st6[:, t, :], src[:, t, :])
                e.drain()
                for t in range(G):
                    e.bn_aggr(mv[:, t, :], st6[:, t, :])
                e.drain()
                e.tensor_scalar(rs[:, :, :], mv[:, :, 1:2], 1e-5, None, ALU.add)
                return e.tensor_tensor(src[:, :, :], src[:, :, :], mv[:, :, 0:1].broadcast_to(GF), ALU.subtract)

            def ln_tail(dst, src):
                @S_("act")
                def _(e, sem):
                    e.activation(rs[:, :, :], rs[:, :, :], ACT.Sqrt).then_inc(sem, 1)

                @S_("dve")
                def _(e, sem):
                    e.reciprocal(rs[:, :, :], rs[:, :, :])
                    e.drain()
                    e.tensor_tensor(dst[:, :, :], src[:, :, :], rs[:, :, :].broadcast_to(GF), ALU.mult).then_inc(sem, 1)

            def store_x(src):
                @S_("sp", 16)
                def _(e, sem):
                    e.dma_start(x_t[bass.ds(cur["g"], 1)].rearrange("o p t f -> (o p) t f"), src[:, :, :]).then_inc(sem, 16)

            def turned(src, dst, psum):
                @S_("pe")
                def _(e, sem):
                    for t in range(G):
                        last = e.transpose(psum[:, t, :], src[:, t, :], ident[:, :])
                    last.then_inc(sem, 1)

                @S_("act")
                def _(e, sem):
                    e.copy(dst[:, :, :], psum[:, 0:G, :]).then_inc(sem, 1)

            def scatter(src, width, table, gi):
                @S_("pool")
                def _(e, sem):
                    for t in range(G):
                        e.indirect_dma_start(table, bass.IndirectOffsetOnAxis(ap=gi[:, t:t + 1], axis=0),
                                             src[:, t, 0:width], None, bounds_check=DRANKS - 1,
                                             oob_is_err=False).then_inc(s_scat, 16)
                    e.wait_ge(s_scat, (cur["turn"] + 1) * (16 * G))
                    e.sem_inc(sem, 1)

            if layer in (0, 2):
                gi = n("gi", [P, G], I32)
            if layer == 0:
                xT = win[:, 0]
                tab, sd, sd3 = n("tab", [P, G, W1]), n("sd", [P, G, H]), n("sd3", [P, G, 3, H], BF16)

                @S_("pe")
                def _(e, sem):
                    for t in range(G):
                        last = e.matmul(pA[:, 0, t, :], Es[:, t, :], Ar[:, t, :], start=True, stop=True)
                    last.then_inc(sem, 1)

                @S_("dve")
                def _(e, sem):
                    e.tensor_tensor(y[:, :, :], x[:, :, :], pA[:, 0, 0:G, :], ALU.add)
                    e.drain()
                    layernorm(e, y, None).then_inc(sem, 1)
                ln_tail(x, y)
                turned(x, xT, pA[:, 0])
                for part in range(2):
                    tiles = range(4 * part, min(4 * part + 4, G))

                    @S_("pe")
                    def _(e, sem, tiles=tiles):
                        for t in tiles:
                            o = pA[:, 0, :, :].rearrange("p (a b) c -> p a (b c)", b=2)
                            last = e.matmul(o[:, t % 4, :], xT[:, t, :], wn[:, :, :].rearrange("p h d -> p (h d)"),
                                            start=True, stop=True)
                            last = e.matmul(pE[:, t % 4, 0:2 * H], xT[:, t, :], vs[:, :, :].rearrange("p k h -> p (k h)"),
                                            start=True, stop=True)
                        last.then_inc(sem, 1)

                    @S_("dve")
                    def _(e, sem, tiles=tiles):
                        m = len(tiles)
                        ts = slice(tiles[0], tiles[-1] + 1)
                        o = pA[:, 0, :, :].rearrange("p (a b) c -> p a (b c)", b=2)
                        e.tensor_copy(tab[:, ts, 0:H * DH], o[:, 0:m, :])
                        e.tensor_copy(tab[:, ts, H * DH:W1], pE[:, 0:m, 0:H])
                        last = e.tensor_copy(sd[:, ts, :], pE[:, 0:m, H:2 * H])
                        if tiles[0]:
                            e.tensor_copy(gi[:, :], grank[:, bass.ds(cur["g"] * G, G)])
                            e.drain()
                            e.tensor_copy(sd3[:, :, 0, :], sd[:, :, :])
                            for part in (1, 2):
                                e.drain()
                                e.tensor_tensor(sd[:, :, :], sd[:, :, :], sd3[:, :, part - 1, :], ALU.subtract)
                                e.drain()
                                last = e.tensor_copy(sd3[:, :, part, :], sd[:, :, :])
                        last.then_inc(sem, 1)

                @S_("sp", 32)
                def _(e, sem):
                    e.dma_start(x_t[bass.ds(cur["g"], 1)].rearrange("o p t f -> (o p) t f"), x[:, :, :]).then_inc(sem, 16)
                    e.dma_start(d["t1"].rearrange("(g t p) f -> g p t f", t=G, p=P)[bass.ds(cur["g"], 1)]
                                .rearrange("o p t f -> (o p) t f"), tab[:, :, :]).then_inc(sem, 16)
                scatter(sd3[:, :, :, :].rearrange("p t k h -> p t (k h)"), 3 * H, d["sd"], gi)
            if layer == 1:
                cc = n("cc", [P, G, K])
                ccT = n("ccT", [P, 2, G * P])
                hid = win[:, :, :, :].rearrange("p k t f -> p k (t f)")
                xT = Es

                @S_("pe")
                def _(e, sem):
                    for t in range(G):
                        for k in range(2):
                            last = e.matmul(pA[:, k, t, :], Es[:, t, :], Ar[:, t, k * F:(k + 1) * F], start=True, stop=True)
                    last.then_inc(sem, 1)

                @S_("act")
                def _(e, sem):
                    for k in range(2):
                        last = e.activation(cc[:, :, k * F:(k + 1) * F], pA[:, k, 0:G, :], ACT.Relu)
                    last.then_inc(sem, 1)

                @S_("pe")
                def _(e, sem):
                    for t in range(G):
                        for k in range(2):
                            last = e.transpose(pA[:, k, t, :], cc[:, t, k * F:(k + 1) * F], ident[:, :])
                    last.then_inc(sem, 1)

                @S_("act")
                def _(e, sem):
                    for k in range(2):
                        last = e.copy(ccT[:, k, :], pA[:, k, 0:G, :].rearrange("p t f -> p (t f)"))
                    last.then_inc(sem, 1)

                @S_("pe")
                def _(e, sem):
                    for j in range(2):
                        o = pA[:, j].rearrange("p t f -> p (t f)")
                        for lo_, hi_ in ((0, 4 * P), (4 * P, G * P)):
                            for k in range(2):
                                last = e.matmul(o[:, lo_:hi_], w1[:, k, j * F:(j + 1) * F], ccT[:, k, lo_:hi_],
                                                start=(k == 0), stop=(k == 1))
                    last.then_inc(sem, 1)

                @S_("act")
                def _(e, sem):
                    for j in range(2):
                        last = e.activation(hid[:, j, :], pA[:, j, 0:G, :].rearrange("p t f -> p (t f)"), ACT.Relu,
                                            bias=b1[:, j:j + 1])
                    last.then_inc(sem, 1)

                @S_("pe")
                def _(e, sem):
                    for t in range(G):
                        for j in range(2):
                            last = e.matmul(pA[:, 0, t, :], hid[:, j, t * P:(t + 1) * P], w2[:, j, :],
                                            start=(j == 0), stop=(j == 1))
                    last.then_inc(sem, 1)

                @S_("dve")
                def _(e, sem):
                    e.tensor_tensor(y[:, :, :], x[:, :, :], pA[:, 0, 0:G, :], ALU.add)
                    e.drain()
                    e.tensor_tensor(y[:, :, :], y[:, :, :], b2[:, :].unsqueeze(1).broadcast_to(GF), ALU.add)
                    e.drain()
                    layernorm(e, y, None).then_inc(sem, 1)
                ln_tail(x, y)
                turned(x, xT, pE)

                @S_("pe")
                def _(e, sem):
                    for t in range(G):
                        last = e.matmul(pE[:, t, :], xT[:, t, :], wg[:, :], start=True, stop=True)
                    last.then_inc(sem, 1)

                @S_("dve")
                def _(e, sem):
                    e.tensor_tensor(y[:, :, :], pE[:, 0:G, :],
                                    dinv[:, bass.ds(cur["g"] * G, G)].unsqueeze(2).broadcast_to(GF),
                                    ALU.mult).then_inc(sem, 1)

                @S_("sp", 32)
                def _(e, sem):
                    e.dma_start(x_t[bass.ds(cur["g"], 1)].rearrange("o p t f -> (o p) t f"), x[:, :, :]).then_inc(sem, 16)
                    e.dma_start(d["t2"].rearrange("(g t p) f -> g p t f", t=G, p=P)[bass.ds(cur["g"], 1)]
                                .rearrange("o p t f -> (o p) t f"), y[:, :, :]).then_inc(sem, 16)
            if layer == 2:
                own = ET
                xT = win[:, 0]
                ta, tb = y, Ar

                @S_("pe")
                def _(e, sem):
                    for t in range(G):
                        last = e.matmul(pA[:, 0, t, :], Es[:, t, :], Ar[:, t, :], start=True, stop=True)
                    last.then_inc(sem, 1)

                @S_("sp", 16)
                def _(e, sem):
                    e.dma_start(own[:, :, :], d["t2"].rearrange("(g t p) f -> g p t f", t=G, p=P)[bass.ds(cur["g"], 1)]
                                .rearrange("o p t f -> (o p) t f")).then_inc(sem, 16)

                @S_("dve")
                def _(e, sem):
                    e.tensor_tensor(y[:, :, :], own[:, :, :], pA[:, 0, 0:G, :], ALU.add)
                    e.drain()
                    e.tensor_tensor(y[:, :, :], y[:, :, :],
                                    dinv[:, bass.ds(cur["g"] * G, G)].unsqueeze(2).broadcast_to(GF), ALU.mult)
                    e.drain()
                    e.tensor_tensor(y[:, :, :], y[:, :, :], b2[:, :].unsqueeze(1).broadcast_to(GF), ALU.add).then_inc(sem, 1)

                @S_("act")
                def _(e, sem):
                    e.activation(y[:, :, :], y[:, :, :], ACT.Gelu).then_inc(sem, 1)

                @S_("dve")
                def _(e, sem):
                    e.tensor_tensor(y[:, :, :], x[:, :, :], y[:, :, :], ALU.add)
                    e.drain()
                    layernorm(e, y, None).then_inc(sem, 1)
                ln_tail(x, y)
                turned(x, xT, pA[:, 0])

                @S_("pe")
                def _(e, sem):
                    for t in range(G):
                        e.matmul(pA[:, 0, t, :], xT[:, t, :], we[:, 0, :], start=True, stop=True)
                        last = e.matmul(pE[:, t, :], xT[:, t, :], we[:, 1, :], start=True, stop=True)
                    last.then_inc(sem, 1)

                @S_("dve")
                def _(e, sem):
                    e.tensor_copy(ta[:, :, :], pA[:, 0, 0:G, :])
                    e.tensor_tensor(tb[:, :, :], pE[:, 0:G, :], be[:, :].unsqueeze(1).broadcast_to(GF), ALU.add)
                    e.tensor_copy(gi[:, :], grank[:, bass.ds(cur["g"] * G, G)]).then_inc(sem, 1)

                @S_("sp", 32)
                def _(e, sem):
                    e.dma_start(x_t[bass.ds(cur["g"], 1)].rearrange("o p t f -> (o p) t f"), x[:, :, :]).then_inc(sem, 16)
                    e.dma_start(d["t3"].rearrange("(g t p) f -> g p t f", t=G, p=P)[bass.ds(cur["g"], 1)]
                                .rearrange("o p t f -> (o p) t f"), ta[:, :, :]).then_inc(sem, 16)
                scatter(tb, F, d["bd"], gi)
            if layer == 3:
                flat = lambda t: t.rearrange("p t f -> p (t f)")
                xT, aT = ET, win[:, 0]
                mT, uT = Ar, Es
                dg = n("dg", [1, G * P])
                halves = ((0, 4 * P), (4 * P, G * P))

                @S_("sp", 16)
                def _(e, sem):
                    e.dma_start(dg[:, :], d["deg"].rearrange("(g t) p -> g (t p)", t=G)[bass.ds(cur["g"], 1), :]).then_inc(sem, 16)

                @S_("pe")
                def _(e, sem):
                    for t in range(G):
                        e.matmul(pA[:, 0, t, :], Ar[:, t, :], Es[:, t, :], start=True, stop=True)
                        last = e.transpose(pE[:, t, :], x[:, t, :], ident[:, :])
                    last.then_inc(sem, 1)

                @S_("act")
                def _(e, sem):
                    e.copy(aT[:, :, :], pA[:, 0, 0:G, :])
                    e.copy(xT[:, :, :], pE[:, 0:G, :]).then_inc(sem, 1)

                @S_("pe")
                def _(e, sem):
                    for lo_, hi_ in halves:
                        o = flat(pA[:, 0])[:, lo_:hi_]
                        e.matmul(o, we2[:, :], flat(aT[:, :, :])[:, lo_:hi_], start=True, stop=False)
                        last = e.matmul(o, be2[:, :], dg[:, lo_:hi_], start=False, stop=True)
                    last.then_inc(sem, 1)

                @S_("act")
                def _(e, sem):
                    e.copy(mT[:, :, :], pA[:, 0, 0:G, :]).then_inc(sem, 1)

                @S_("pe")
                def _(e, sem):
                    for lo_, hi_ in halves:
                        o = flat(pE[:, :, :])[:, lo_:hi_]
                        e.matmul(o, wu[:, 0, :], flat(xT[:, :, :])[:, lo_:hi_], start=True, stop=False)
                        last = e.matmul(o, wu[:, 1, :], flat(mT[:, :, :])[:, lo_:hi_], start=False, stop=True)
                    last.then_inc(sem, 1)

                @S_("act")
                def _(e, sem):
                    e.activation(uT[:, :, :], pE[:, 0:G, :], ACT.Gelu, bias=bu[:, 0:1]).then_inc(sem, 1)

                @S_("pe")
                def _(e, sem):
                    for t in range(G):
                        last = e.matmul(pA[:, 0, t, :], uT[:, t, :], wu2[:, :], start=True, stop=True)
                    last.then_inc(sem, 1)

                @S_("dve")
                def _(e, sem):
                    e.tensor_tensor(y[:, :, :], x[:, :, :], pA[:, 0, 0:G, :], ALU.add)
                    e.drain()
                    e.tensor_tensor(y[:, :, :], y[:, :, :], b2[:, :].unsqueeze(1).broadcast_to(GF), ALU.add)
                    e.drain()
                    layernorm(e, y, None).then_inc(sem, 1)
                ln_tail(y, y)

                @S_("dve")
                def _(e, sem):
                    e.tensor_tensor(y[:, :, :], y[:, :, :], gam[:, :].unsqueeze(1).broadcast_to(GF), ALU.mult)
                    e.drain()
                    e.tensor_tensor(y[:, :, :], y[:, :, :], bet[:, :].unsqueeze(1).broadcast_to(GF), ALU.add)
                    e.drain()
                    e.tensor_tensor(y[:, :, :], y[:, :, :], x[:, :, :], ALU.add)
                    e.drain()
                    layernorm(e, y, None).then_inc(sem, 1)
                ln_tail(y, y)
                store_x(y)
            return stages, sm

        cur = {}
        chains = [make_chain(ci) for ci in range(nchain)]
        block = ctx.enter_context(nc.Block())

        def run(e, name):
            e.wait_ge(s_z, 1)
            with e.Fori(0, NG // nchain) as it:
                for k in range(max(len(st) for st, _ in chains)):
                    for ci, (st, sm) in enumerate(chains):
                        cur["g"], cur["turn"] = it * nchain + ci, it
                        one_stage(e, name, st, k, it, sm, s_held)

        @block.sync
        def _(e):
            for t, ap in loads:
                e.dma_start(t.ap(), ap, allow_slow_non_contiguous=True).then_inc(s_w, 16)
            e.wait_ge(s_w, 16 * len(loads))
            if layer == 0:
                e.wait_ge(s_p2, 1)
            for _, sm in chains:
                e.sem_inc(sm, 1)
            e.sem_inc(s_z, 1)
            run(e, "sp")
            if layer == 3:
                for st, sm in chains:
                    e.wait_ge(sm, NG // nchain * sum(w for _, w, _ in st) + 1)
                e.dma_start(out, d["x"][0:N, :]).then_inc(s_p, 16)
                e.wait_ge(s_p, 16)
            else:
                for st, sm in chains:
                    e.wait_ge(sm, NG // nchain * sum(w for _, w, _ in st) + 1)

        @block.tensor
        def _(e):
            if layer == 0:
                e.wait_ge(s_w, 16 * len(loads))
                for h in range(H):
                    for k in range(2):
                        last = e.matmul(vps[0][:, k * H + h:k * H + h + 1], wnT[:, h, :], a2[:, k, h:h + 1],
                                        start=True, stop=True)
                last.then_inc(s_p, 1)
            run(e, "pe")

        @block.vector
        def _(e):
            if layer == 0:
                e.wait_ge(s_p, 1)
                e.tensor_copy(vs[:, :, :].rearrange("p k h -> p (k h)"), vps[0]).then_inc(s_p2, 1)
            run(e, "dve")

        @block.scalar
        def _(e):
            run(e, "act")

        if layer in (0, 2):
            @block.gpsimd
            def _(e):
                run(e, "pool")


def one_stage(eng, name, stages, k, turn, sem, held):
    if k >= len(stages) or stages[k][0] != name:
        return
    total = sum(w for _, w, _ in stages)
    eng.wait_ge(sem, turn * total + sum(w for _, w, _ in stages[:k]) + 1)
    if name != "sp":
        eng.sem_inc(held, 1)
    stages[k][2](eng, sem)


_INS = ["x", "src", "dst", "edge_weight", "L0_gnn_W", "L1_gnn_W_n", "L1_gnn_a_src", "L1_gnn_a_dst",
        "L1_gnn_mlp_W1", "L1_gnn_mlp_b1", "L1_gnn_mlp_W2", "L1_gnn_mlp_b2", "L2_gnn_W", "L2_gnn_b",
        "L3_gnn_We1", "L3_gnn_be1", "L3_gnn_We2", "L3_gnn_be2", "L3_gnn_Wu1", "L3_gnn_bu1", "L3_gnn_Wu2",
        "L3_gnn_bu2", "L3_gnn_gamma", "L3_gnn_beta"]
STOP, DEBUG = 99, False


def kernel(**inputs):
    import numpy as np
    import concourse.bacc as bacc
    from concourse.bass_utils import run_bass_kernel_spmd

    nc = bacc.Bacc("TRN2", target_bir_lowering=False, num_devices=1)
    arrays, a = {}, {}
    for name in _INS:
        v = np.ascontiguousarray(inputs[name])
        arrays[f"in_{name}"] = v
        a[name] = nc.dram_tensor(f"in_{name}", v.shape, mybir.dt.from_np(v.dtype), kind="ExternalInput").ap()
    wt = np.ascontiguousarray(np.transpose(np.asarray(inputs["L1_gnn_W_n"]), (2, 0, 1)))
    arrays["in_WnT"] = wt
    a["WnT"] = nc.dram_tensor("in_WnT", wt.shape, F32, kind="ExternalInput").ap()
    at = np.ascontiguousarray(np.transpose(np.stack([np.asarray(inputs["L1_gnn_a_src"]),
                                                     np.asarray(inputs["L1_gnn_a_dst"])]), (2, 0, 1)))
    arrays["in_aT"] = at
    a["aT"] = nc.dram_tensor("in_aT", at.shape, F32, kind="ExternalInput").ap()
    out = nc.dram_tensor("out_0", (N, F), F32, kind="ExternalOutput").ap()
    prog(nc, a, out, STOP, DEBUG)
    r = run_bass_kernel_spmd(nc, [arrays], core_ids=[0])
    return r.results[0]["out_0"]
```

```python
from contextlib import ExitStack

import concourse.bass as bass
from concourse import mybir

F32 = mybir.dt.float32
BF16 = mybir.dt.bfloat16
I32 = mybir.dt.int32
U8 = mybir.dt.uint8
ALU = mybir.AluOpType
ACT = mybir.ActivationFunctionType
AX = mybir.AxisListType

P = 128
N = 12500
F = 128
E = 200000
H = 4
DH = 64
NT = -(-N // P)
NP = NT * P
NLAST = N - (NT - 1) * P
NB = 16
EB = NB * P
B = -(-E // EB)
ELAST = E - (B - 1) * EB
PAD_NODE = NP - 1
RANKS = N + 4 * P + 4
DRANKS = NP + 2 * P
BIG = 1.0e30
G = 7
NG = NT // G
META = 5
W0, W1 = F + 1, H * DH + H
assert NT % G == 0 and (B - 2) % 6 == 0 and B <= P


def one_hot(eng, out, iota, index, weight=None):
    if weight is None:
        return eng.tensor_scalar(out, iota, index, None, ALU.is_equal)
    return eng.tensor_scalar(out, iota, index, weight, ALU.is_equal, ALU.mult)


def prog(nc, a, out):
    def dram(name, shape, dt):
        return nc.dram_tensor(name, shape, dt, kind="Internal").ap()

    meta_d = dram("meta_d", (B, P, META, NB), F32)
    pen_d = dram("pen_d", (B, NB, P + 1), F32)
    rowpen_d = dram("rowpen_d", (B, 2, H * (NB + 1)), F32)
    lrrow_d = dram("lrrow_d", (B, EB), U8)
    base_d = dram("base_d", (B, NB), I32)
    rel_d = dram("rel_d", (B, NB), I32)
    qbase_d = dram("qbase_d", (B, NB // 4), I32)
    wflat_d = dram("wflat_d", (B, EB), F32)
    t0_d = dram("t0_d", (NP, W0), F32)
    t1_d = dram("t1_d", (NP, W1), F32)
    t2_d = dram("t2_d", (NP, F), F32)
    t3_d = dram("t3_d", (NP, F), F32)
    x_d = dram("x_d", (NP, F), F32)
    sd_d = dram("sd_d", (DRANKS, 3 * H), BF16)
    bd_d = dram("bd_d", (DRANKS, F), F32)
    rb_d = dram("rb_d", (NT, 1), I32)
    deg_d = dram("deg_d", (NT, P), F32)
    lrn_d = dram("lrn_d", (NT, P), BF16)

    with ExitStack() as top:
        def sb(name, shape, dt=F32, ctx=top):
            return ctx.enter_context(nc.sbuf_tensor(name, shape, dt))

        iota = sb("iota", [P, P])
        iotab = sb("iotab", [P, P], BF16)
        iotap = sb("iotap", [P, 1])
        ident = sb("ident", [P, P])
        ones = sb("ones", [P, P])
        grank = sb("grank", [P, NT])
        dinv = sb("dinv", [P, NT])

        with ExitStack() as ctx:
            def s(name, shape, dt=F32):
                return sb(name, shape, dt, ctx)

            ii = s("ii", [P, P], I32)
            tri = s("tri", [P, P])
            ip = s("ip", [P, 1], I32)
            dsti = s("dsti", [B, EB], I32)
            srci = s("srci", [B, EB], I32)
            wrow = s("wrow", [B, EB])
            edge = {c: s(f"edge{c}", [B, EB]) for c in (0, 1, 3, 4)}
            edge[2] = wrow
            dstf = s("dstf", [B, EB])
            hii = s("hii", [B, EB], I32)
            prevl = s("prevl", [B, 1], I32)
            nextf = s("nextf", [B, 1], I32)
            pl = s("pl", [B, 2])
            start = s("start", [B, EB])
            pen = s("pen", [B, NB, P + 1])
            rowpen = s("rowpen", [B, 2, H, NB + 1])
            cum = s("cum", [B, EB])
            bf = s("bf", [B, NB])
            bi = s("bi", [B, NB], I32)
            ri = s("ri", [B, NB], I32)
            qi = s("qi", [B, NB // 4], I32)
            off = s("off", [B, 1])
            lrb = s("lrb", [B, EB], U8)
            meta = s("meta", [P, B, META, NB])
            zero = s("zero", [P, 1024])
            tp = [ctx.enter_context(nc.psum_tensor(f"tp{i}", [P, 4, P], F32)) for i in range(2)]
            offp = ctx.enter_context(nc.psum_tensor("offp", [P, 1], F32))
            sem = lambda n: ctx.enter_context(nc.semaphore(n))
            s_iota, s_pad, s_load, s_const = sem("s_iota"), sem("s_pad"), sem("s_load"), sem("s_const")
            s_cum, s_off, s_edge, s_tp, s_ev, s_st = (sem("s_cum"), sem("s_off"), sem("s_edge"), sem("s_tp"),
                                                      sem("s_ev"), sem("s_st"))
            block = ctx.enter_context(nc.Block())
            full = (B - 1) * EB

            @block.gpsimd
            def _(e):
                e.iota(ii[:, :], [[1, P]], base=0, channel_multiplier=0).then_inc(s_iota, 1)
                e.iota(ip[:, :], [[1, 1]], base=0, channel_multiplier=1).then_inc(s_iota, 1)

            @block.sync
            def _(e):
                e.wait_ge(s_pad, 1)
                for t, d in ((dsti, a["dst"]), (srci, a["src"]), (wrow, a["edge_weight"])):
                    e.dma_start(t[0:B - 1, :], d[0:full].rearrange("(b e) -> b e", e=EB)).then_inc(s_load, 16)
                    e.dma_start(t[B - 1:B, 0:ELAST], d[full:E].rearrange("(b e) -> b e", b=1)).then_inc(s_load, 16)
                d = a["dst"]
                e.dma_start(prevl[1:B, :], d[0:full].rearrange("(b e) -> b e", e=EB)[:, EB - 1:EB],
                            allow_slow_non_contiguous=True).then_inc(s_load, 16)
                e.dma_start(nextf[0:B - 2, :],
                            d[EB:full].rearrange("(b e) -> b e", e=EB)[:, 0:1],
                            allow_slow_non_contiguous=True).then_inc(s_load, 16)
                e.dma_start(nextf[B - 2:B - 1, :],
                            d[full:full + 1].rearrange("(b e) -> b e", b=1)).then_inc(s_load, 16)
                for k in range(DRANKS // P):
                    e.dma_start(bd_d[k * P:(k + 1) * P, :], zero[:, 0:F]).then_inc(s_st, 16)
                e.dma_start(sd_d.rearrange("(p k) h -> p (k h)", p=P),
                            zero[:, 0:DRANKS // P * 3 * H // 2].bitcast(BF16)).then_inc(s_st, 16)
                e.wait_ge(s_edge, 3)
                e.dma_start(base_d, bi[:, :]).then_inc(s_st, 16)
                e.dma_start(rel_d, ri[:, :]).then_inc(s_st, 16)
                e.dma_start(qbase_d, qi[:, :]).then_inc(s_st, 16)
                e.dma_start(wflat_d, wrow[:, :]).then_inc(s_st, 16)
                e.dma_start(pen_d, pen[:, :, :]).then_inc(s_st, 16)
                e.dma_start(rowpen_d.rearrange("b d k -> b (d k)"),
                            rowpen[:, :, :, :].rearrange("b d h k -> b (d h k)")).then_inc(s_st, 16)
                e.dma_start(lrrow_d, lrb[:, :]).then_inc(s_st, 16)
                e.wait_ge(s_ev, META * NB // 4)
                e.dma_start(meta_d.rearrange("b p c t -> p b (c t)"),
                            meta[:, :, :, :].rearrange("p b c t -> p b (c t)")).then_inc(s_st, 16)
                e.wait_ge(s_st, 16 * (DRANKS // P + 1 + 8))

            @block.vector
            def _(e):
                e.memset(zero[:, :], 0.0)
                e.memset(dsti[:, :], PAD_NODE)
                e.memset(srci[:, :], 0)
                e.memset(wrow[:, :], 0.0)
                e.memset(prevl[:, :], -1)
                e.memset(nextf[:, :], PAD_NODE)
                e.memset(ones[:, :], 1.0)
                e.drain().then_inc(s_pad, 1)
                e.wait_ge(s_iota, 2)
                e.tensor_copy(iota[:, :], ii[:, :])
                e.tensor_copy(iotab[:, :], ii[:, :])
                e.tensor_copy(iotap[:, :], ip[:, :])
                e.drain()
                one_hot(e, ident[:, :], iota[:, :], iotap[:, 0:1])
                e.tensor_scalar(tri[:, :], iota[:, :], iotap[:, 0:1], None, ALU.is_gt)
                e.drain().then_inc(s_const, 1)
                e.wait_ge(s_load, 16 * 9)
                e.tensor_copy(dstf[:, :], dsti[:, :])
                e.tensor_copy(edge[0][:, :], srci[:, :])
                e.tensor_scalar(hii[:, :], dsti[:, :], 7, None, ALU.arith_shift_right)
                e.tensor_copy(pl[:, 0:1], prevl[:, :])
                e.tensor_copy(pl[:, 1:2], nextf[:, :])
                e.drain()
                e.tensor_copy(edge[3][:, :], hii[:, :])
                e.tensor_tensor(start[:, 1:EB], dstf[:, 1:EB], dstf[:, 0:EB - 1], ALU.not_equal)
                e.tensor_tensor(start[:, 0:1], dstf[:, 0:1], pl[:, 0:1], ALU.not_equal)
                e.drain()
                e.scalar_tensor_tensor(edge[4][:, :], edge[3][:, :], -float(P), dstf[:, :], ALU.mult, ALU.add)
                e.tensor_tensor_scan(cum[:, :], start[:, :], start[:, :], 0.0, ALU.add, ALU.max)
                st = start[:, :].rearrange("b (t e) -> b t e", e=P)
                e.tensor_scalar(pen[:, :, 0:P], st, -BIG, None, ALU.mult)
                e.tensor_scalar(pen[:, 0:NB - 1, P:P + 1], st[:, 1:NB, 0:1], -BIG, None, ALU.mult)
                e.tensor_tensor(pl[:, 0:1], pl[:, 1:2], dstf[:, EB - 1:EB], ALU.not_equal)
                e.drain().then_inc(s_cum, 1)
                e.tensor_scalar(pen[:, NB - 1, P:P + 1], pl[:, 0:1], -BIG, None, ALU.mult)
                e.memset(rowpen[:, :, :, :], -BIG)
                ct = cum[:, :].rearrange("b (t e) -> b t e", e=P)
                e.tensor_tensor(edge[1][:, :].rearrange("b (t e) -> b t e", e=P), ct,
                                ct[:, :, 0:1].broadcast_to([B, NB, P]), ALU.subtract)
                e.drain()
                e.tensor_copy(lrb[:, :], edge[1][:, :])
                for h in range(H):
                    e.tensor_reduce(rowpen[:, 0, h, 1:NB + 1], pen[:, :, 0:P], AX.X, ALU.min)
                    e.tensor_reduce(rowpen[:, 1, h, 0:NB], pen[:, :, 1:P + 1], AX.X, ALU.min)
                e.wait_ge(s_off, 1)
                e.tensor_copy(off[:, :], offp[0:B, :])
                e.drain()
                e.tensor_scalar(bf[:, :], ct[:, :, 0], off[:, 0:1], -1.0, ALU.add, ALU.add)
                e.drain()
                e.tensor_copy(bi[:, :], bf[:, :])
                bq = bf[:, :].rearrange("b (q j) -> b q j", j=4)
                e.tensor_copy(qi[:, :], bq[:, :, 0])
                e.tensor_tensor(ri[:, :].rearrange("b (q j) -> b q j", j=4), bq,
                                bq[:, :, 0:1].broadcast_to([B, NB // 4, 4]), ALU.subtract)
                e.drain().then_inc(s_edge, 3)
                for k in range(META * NB // 4):
                    c, q = divmod(k, NB // 4)
                    e.wait_ge(s_tp, k + 1)
                    dstv = meta[:, :, c, 4 * q:4 * q + 4]
                    if c == 0:
                        dstv = meta[:, :, :, :].bitcast(I32)[:, :, c, 4 * q:4 * q + 4]
                    e.tensor_copy(dstv, tp[k % 2][:, :, 0:B].rearrange("p t b -> p b t")).then_inc(s_ev, 1)

            @block.tensor
            def _(e):
                e.wait_ge(s_cum, 1)
                e.wait_ge(s_const, 1)
                e.matmul(offp[0:B, :], tri[0:B, 0:B], cum[:, EB - 1:EB], start=True, stop=True).then_inc(s_off, 1)
                e.wait_ge(s_edge, 3)
                for k in range(META * NB // 4):
                    c, q = divmod(k, NB // 4)
                    if k >= 2:
                        e.wait_ge(s_ev, k - 1)
                    for j in range(4):
                        t = 4 * q + j
                        last = e.transpose(tp[k % 2][:, j, 0:B], edge[c][:, t * P:(t + 1) * P], ident[0:B, 0:B])
                    last.then_inc(s_tp, 1)

        with ExitStack() as ctx:
            xs = sb("xs", [P, NT, W0], F32, ctx)
            xw = sb("xw", [P, NT, F], F32, ctx)
            wb = sb("wb", [P, F], F32, ctx)
            s_z, s_x, s_sc, s_o = (ctx.enter_context(nc.semaphore(n)) for n in ("s_z", "s_x", "s_sc", "s_o"))
            block = ctx.enter_context(nc.Block())

            @block.sync
            def _(e):
                e.wait_ge(s_z, 1)
                e.dma_start(xs[:, 0:NT - 1, 0:F],
                            a["x"][0:(NT - 1) * P, :].rearrange("(t p) f -> p t f", p=P)).then_inc(s_x, 16)
                e.dma_start(xs[0:NLAST, NT - 1, 0:F], a["x"][(NT - 1) * P:N, :]).then_inc(s_x, 16)
                e.dma_start(wb[:, :], a["L0_gnn_W"][0:1, :].broadcast_to([P, F])).then_inc(s_x, 16)
                e.wait_ge(s_sc, 1)
                e.dma_start(t0_d.rearrange("(t p) f -> p t f", p=P), xs[:, :, :]).then_inc(s_o, 16)
                e.dma_start(x_d.rearrange("(t p) f -> p t f", p=P), xs[:, :, 0:F]).then_inc(s_o, 16)
                e.wait_ge(s_o, 32)

            @block.vector
            def _(e):
                e.memset(xs[:, NT - 1, :], 0.0)
                e.drain().then_inc(s_z, 1)
                e.wait_ge(s_x, 48)
                e.tensor_tensor(xw[:, :, :], xs[:, :, 0:F], wb[:, :].unsqueeze(1).broadcast_to([P, NT, F]), ALU.mult)
                e.drain()
                e.tensor_reduce(xs[:, :, F:F + 1], xw[:, :, :], AX.X, ALU.add)
                e.drain().then_inc(s_sc, 1)

        held = top.enter_context(nc.semaphore("s_held"))
        consts = dict(held=held, iota=iota, iotab=iotab, iotap=iotap, ident=ident, ones=ones)
        d = dict(meta=meta_d, pen=pen_d, rowpen=rowpen_d, lrrow=lrrow_d, base=base_d, rel=rel_d, qbase=qbase_d,
                 wflat=wflat_d, rb=rb_d, deg=deg_d, lrn=lrn_d, x=x_d, t1=t1_d, t2=t2_d, t3=t3_d, sd=sd_d, bd=bd_d)

        with ExitStack() as ctx:
            acc = sb("acc0", [P, 1, RANKS], F32, ctx)
            den = sb("den0", [3, RANKS], F32, ctx)
            with nc.psum_tensor("hist", [NT, P], F32) as hist:
                edge_pass(nc, sb, "soft1", t0_d, W0, acc, den, hist, consts, d)
                node_map(nc, sb, hist, consts, grank, dinv, rb_d, deg_d, lrn_d)
            node_pass(nc, sb, 0, acc, den, grank, dinv, consts, a, d, out)
        with ExitStack() as ctx:
            acc = sb("acc1", [P, 2, RANKS], F32, ctx)
            den = sb("den1", [3 * H, RANKS], F32, ctx)
            edge_pass(nc, sb, "soft4", t1_d, W1, acc, den, None, consts, dict(d, dst=sd_d))
            node_pass(nc, sb, 1, acc, den, grank, dinv, consts, a, d, out)
        with ExitStack() as ctx:
            acc = sb("acc2", [P, 1, RANKS], F32, ctx)
            edge_pass(nc, sb, "sum", t2_d, F, acc, None, None, consts, d)
            node_pass(nc, sb, 2, acc, None, grank, dinv, consts, a, d, out)
        with ExitStack() as ctx:
            acc = sb("acc3", [P, 1, RANKS], F32, ctx)
            edge_pass(nc, sb, "mlp", t3_d, F, acc, None, None,
                      dict(consts, crow=a["L3_gnn_We1"][2 * F:2 * F + 1, :]), dict(d, dst=bd_d))
            node_pass(nc, sb, 3, acc, None, grank, dinv, consts, a, d, out)


class Batch:

    def __init__(self, U, off, it=0):
        self.b, self.par, self.turn = it * U + off, off % U, it + off // U


def batches(eng, U, body):
    body(None, Batch(U, 0))
    body(Batch(U, 0), Batch(U, 1))
    with eng.Fori(0, (B - 2) // U) as it:
        for i in range(U):
            body(Batch(U, 1 + i, it), Batch(U, 2 + i, it))
    body(Batch(U, B - 1), None)


def each_batch(eng, U, body):
    body(Batch(U, 0))
    body(Batch(U, 1))
    with eng.Fori(0, (B - 2) // U) as it:
        for i in range(U):
            body(Batch(U, 2 + i, it))


def load_values(nc, engine, ap, most):
    _, v = nc.values_load_multi_w_load_instructions(ap, engines=(engine,), min_val=0, max_val=most,
                                                    skip_runtime_bounds_check_because="no rank is above N")
    return v


def edge_pass(nc, sb, mode, table, width, acc, den, hist, c, d):
    soft = mode in ("soft1", "soft4")
    heads = H if mode == "soft4" else 1
    dst_w = {"soft4": 3 * H, "mlp": F}.get(mode, 0)
    R = heads * NB
    K1 = NB + 1
    blocks = 2 if mode == "soft4" else 1
    n_ld = (heads + 1 if soft else 0) + (1 + NB if dst_w else 0) + (mode == "mlp")
    NQ = NB // 4
    U = 2 if mode == "soft4" else 3
    NS = 2 if mode == "soft4" else 4
    NLRB = 1 if soft else U
    PE, DVE, SP = mybir.EngineType.PE, mybir.EngineType.DVE, mybir.EngineType.SP
    iota, ident, ones = c["iota"], c["ident"], c["ones"]
    with ExitStack() as ctx:
        def s(name, shape, dt=F32):
            return sb(f"{name}_{mode}", shape, dt, ctx)

        def ps(name, shape):
            return ctx.enter_context(nc.psum_tensor(f"{name}_{mode}", shape, F32))

        def sem(name):
            return ctx.enter_context(nc.semaphore(f"{name}_{mode}"))

        rows = s("rows", [P, U, NB, width])
        idx = s("idx", [P, U, NB])
        mt = s("mt", [P, U, META - 1, NB])
        S = s("S", [P, NS, 4, P])
        zb = s("zb", [P, 512], BF16)
        if soft:
            Sb = s("Sb", [P, NS, 4, P], BF16)
            pen = s("pen", [R, U, P + 1])
            rowpen = s("rowpen", [1, U, 2, heads * K1])
            sc = s("sc", [P, heads, NB])
            f1, f2, b1 = (s(n, [R, P]) for n in ("f1", "f2", "b1"))
            m, wr = f1, b1
            col = s("col", [R, 2])
            R_, I_, RB_, J_ = (s(n, [1, heads, K1]) for n in ("Rr", "Ir", "RBr", "Jr"))
            al = s("al", [1, heads])
            if heads > 1:
                line = s("line", [1, R])
            alpha = s("alpha", [P, U, blocks])
            alphad = s("alphad", [3 * heads, U])
            al3 = s("al3", [1, 3, heads])
            wc = s("wc", [P, U, heads, NB])
            rest = s("rest", [P, heads, NB])
            w3 = s("w3", [P, U, NB, 3, heads], BF16)
            scT = ps("scT", [R, P])
            small = ps("small", [P, 512])
            rp1, rp2, cp1, cp2 = small[0:1, 0:R], small[0:1, 64:64 + R], small[0:R, 128:129], small[0:R, 132:133]
            ap, adp = small[:, 136:136 + blocks], small[0:3 * heads, 140:141]
            ex, wp = small[:, 192:192 + R], small[:, 256:256 + R]
            pd = [ps(f"pd{i}", [3 * heads, 512]) for i in range(2)]
        if mode == "soft1":
            ho = s("ho", [P, NS, 4, NT], BF16)
            lo = s("lo", [P, NS, 4, P], BF16)
        if dst_w:
            lrb = s("lrb", [P, NLRB, EB], U8)
            dw = s("dw", [P, U, NB, dst_w], BF16 if soft else F32)
            ST = s("ST", [P, 2, 4, P], BF16 if soft else F32)
        if mode == "mlp":
            wrow = s("wrow", [1, U, EB])
            crow = s("crow", [1, F])
            pre = [ps(f"pre{i}", [P, 4, P]) for i in range(2)]
        pn = [ps(f"pn{i}", [P, blocks, 512]) for i in range(2)]
        s_ld = [sem(f"s_ld{i}") for i in range(U if n_ld else 0)]
        s_ix = [sem(f"s_ix{i}") for i in range(U)]
        s_md = [sem(f"s_md{i}") for i in range(U)]
        s_g = [sem(f"s_g{i}") for i in range(U)]
        if mode == "soft4":
            s_rs = sem("s_rs")
        s_k = c["held"]
        s_init, s_A, s_S, s_mm, s_add = sem("s_init"), sem("s_A"), sem("s_S"), sem("s_mm"), sem("s_add")
        if soft:
            s_Sb = sem("s_Sb")
        if dst_w:
            s_st, s_ex = sem("s_st"), sem("s_ex")
        if mode == "mlp":
            s_pre, s_c = sem("s_pre"), sem("s_c")
        block = ctx.enter_context(nc.Block())

        def a_score(e, bt):
            e.wait_ge(s_g[bt.par], (bt.turn + 1) * (16 * NB))
            g = rows[:, bt.par, :, width - heads:width].rearrange("p t h -> p h t")
            if heads == 1:
                return e.tensor_copy(sc[:, :, :], g)
            e.wait_ge(s_ex, bt.b * NQ + NQ)
            e.tensor_tensor(sc[:, :, :], g, ex.rearrange("p (t h) -> p h t", h=heads), ALU.add)
            e.drain()
            return e.scalar_tensor_tensor(sc[:, :, :], sc[:, :, :], 0.2, sc[:, :, :], ALU.mult, ALU.max)

        def a_scoreT(e, bt):
            return e.transpose(scT[:, :], sc[:, :, :].rearrange("p h t -> p (h t)"), ident[:, :])

        def a_scan1(e, bt):
            e.wait_ge(s_ld[bt.par], (bt.turn + 1) * (16 * n_ld))
            return e.tensor_tensor_scan(f1[:, :], pen[:, bt.par, 0:P], scT[:, :], -BIG, ALU.add, ALU.max)

        def a_rowF(e, bt):
            return e.transpose(rp1, f1[:, P - 1:P], ident[0:R, 0:R])

        def a_scanI(e, bt):
            e.tensor_copy(R_[:, :, 0:1], I_[:, :, NB:K1])
            e.tensor_copy(R_[:, :, 1:K1], rp1.rearrange("o (h t) -> o h t", h=heads))
            e.drain()
            last = e.tensor_tensor_scan(I_[:, :, :].rearrange("o h k -> o (h k)"), rowpen[:, bt.par, 0, :],
                                        R_[:, :, :].rearrange("o h k -> o (h k)"), -BIG, ALU.add, ALU.max)
            return reach(e, last, I_[:, :, 0:NB])

        def reach(e, last, entries):
            if heads == 1:
                return last
            e.drain()
            return e.tensor_copy(line[:, :].rearrange("o (h t) -> o h t", h=heads), entries)

        def a_colI(e, bt):
            return e.transpose(cp1, I_[:, 0, 0:NB] if heads == 1 else line[:, :], ident[0:1, 0:1])

        def a_scan2(e, bt):
            e.tensor_copy(col[:, 0:1], cp1)
            e.drain()
            e.tensor_tensor_scan(f2[:, :], pen[:, bt.par, 0:P], scT[:, :], col[:, 0:1], ALU.add, ALU.max)
            e.drain()
            return e.tensor_tensor_scan(b1[:, ::-1], pen[:, bt.par, P:0:-1], f2[:, ::-1], -BIG, ALU.add, ALU.max)

        def a_rowB(e, bt):
            return e.transpose(rp2, b1[:, 0:1], ident[0:R, 0:R])

        def a_scanJ(e, bt):
            e.tensor_copy(RB_[:, :, 0:NB], rp2.rearrange("o (h t) -> o h t", h=heads))
            e.drain()
            e.tensor_tensor_scan(J_[:, :, :].rearrange("o h k -> o (h k)")[:, ::-1], rowpen[:, bt.par, 1, ::-1],
                                 RB_[:, :, :].rearrange("o h k -> o (h k)")[:, ::-1], -BIG, ALU.add, ALU.max)
            e.drain()
            e.tensor_tensor(al[:, :], R_[:, :, 0], J_[:, :, 0], ALU.subtract)
            e.drain()
            if heads > 1:
                reach(e, None, J_[:, :, 1:K1])
            return e.tensor_scalar(al3[:, :, :], al[:, :].unsqueeze(1).broadcast_to([1, 3, heads]), 0.0, None, ALU.min)

        def a_colJ(e, bt):
            return e.transpose(cp2, J_[:, 0, 1:K1] if heads == 1 else line[:, :], ident[0:1, 0:1])

        def a_alpha(e, bt):
            return e.activation(al3[:, :, :], al3[:, :, :], ACT.Exp)

        def a_alphab(e, bt):
            if heads == 1:
                e.matmul(ap, ones[0:1, :], al3[:, 0, :], start=True, stop=True)
            else:
                for i in range(2):
                    e.matmul(ap[i * DH:(i + 1) * DH, :], ones[0:1, 0:DH], al3[:, 0, i:heads:2], start=True, stop=True)
            return e.transpose(adp, al3[:, :, :].rearrange("o k h -> o (k h)"), ident[0:1, 0:1])

        def a_scan3(e, bt):
            e.tensor_copy(col[:, 1:2], cp2)
            e.tensor_copy(alpha[:, bt.par, :], ap)
            e.tensor_copy(alphad[:, bt.par:bt.par + 1], adp)
            e.drain()
            e.tensor_tensor_scan(m[:, ::-1], pen[:, bt.par, P:0:-1], f2[:, ::-1], col[:, 1:2], ALU.add, ALU.max)
            e.drain()
            return e.tensor_tensor(wr[:, :], scT[:, :], m[:, :], ALU.subtract)

        def a_exp(e, bt):
            return e.activation(wr[:, :], wr[:, :], ACT.Exp)

        def a_wT(e, bt):
            return e.transpose(wp, wr[:, :], ident[0:R, 0:R])

        def a_wc(e, bt):
            return e.copy(wc[:, bt.par, :, :], wp.rearrange("p (h t) -> p h t", h=heads))

        def a_split(e, bt):
            w = wc[:, bt.par, :, :]
            part = [w3[:, bt.par, :, k, :].rearrange("p t h -> p h t") for k in range(3)]
            e.tensor_copy(part[0], w)
            e.drain()
            e.tensor_tensor(rest[:, :, :], w, part[0], ALU.subtract)
            e.drain()
            e.tensor_copy(part[1], rest[:, :, :])
            e.drain()
            return e.tensor_tensor(part[2], rest[:, :, :], part[1], ALU.subtract)

        stages = [("dve", 4, a_score), ("pe", 4, a_scoreT), ("dve", 5, a_scan1), ("pe", 5, a_rowF),
                  ("dve", 6, a_scanI), ("pe", 6, a_colI), ("dve", 8, a_scan2), ("pe", 8, a_rowB),
                  ("dve", 9, a_scanJ), ("pe", 9, a_colJ), ("act", 9, a_alpha), ("pe", 10, a_alphab),
                  ("dve", 12, a_scan3), ("act", 12, a_exp), ("pe", 13, a_wT), ("act", 13, a_wc),
                  ("dve", 15, a_split)]
        NA = {"soft1": len(stages), "soft4": len(stages), "sum": 1, "mlp": NQ}[mode]

        def prepare(e, who, slot, bt):
            for k, (w, sl, fn) in enumerate(stages if soft else []):
                if w == who and sl == slot:
                    e.wait_ge(s_A, (bt.b + U) * NA + k)
                    if who == "pe":
                        e.sem_inc(s_k, 1)
                    fn(e, bt).then_inc(s_A, 1)

        @block.sync
        def _(e):
            if mode == "mlp":
                e.dma_start(crow[:, :], c["crow"]).then_inc(s_c, 16)

            def body(bt):
                e.wait_ge(s_A, (bt.b + 1) * NA)
                e.sem_inc(s_k, 1)
                ld = s_ld[bt.par] if n_ld else None
                e.dma_start(idx[:, bt.par, :], d["meta"][bass.ds(bt.b, 1), :, 0, :].rearrange("o p t -> (o p) t")
                            ).then_inc(s_ix[bt.par], 16)
                if soft:
                    for h in range(heads):
                        e.dma_start(pen[h * NB:(h + 1) * NB, bt.par, :],
                                    d["pen"][bass.ds(bt.b, 1), :, :].rearrange("o t e -> (o t) e")).then_inc(ld, 16)
                    e.dma_start(rowpen[:, bt.par, :, :],
                                d["rowpen"][bass.ds(bt.b, 1), :, 0:heads * K1]).then_inc(ld, 16)
                if mode == "mlp":
                    e.dma_start(wrow[:, bt.par, :], d["wflat"][bass.ds(bt.b, 1), :]).then_inc(ld, 16)
                if dst_w:
                    for q in range(NQ):
                        r0 = load_values(nc, SP, d["base"][bass.ds(bt.b, 1), q * 4:q * 4 + 4], N)
                        for j in range(4):
                            e.dma_start(dw[:, bt.par, q * 4 + j, :], d["dst"][bass.ds(r0[j], P), :]).then_inc(ld, 16)
                    if NLRB == 1:
                        e.wait_ge(s_st, bt.b * NQ + NQ)
                        e.sem_inc(s_k, 1)
                    e.dma_start(lrb[:, bt.par % NLRB, :], d["lrrow"][bass.ds(bt.b, 1), :].broadcast_to([P, EB])).then_inc(ld, 16)
            each_batch(e, U, body)

        @block.gpsimd
        def _(e):
            def body(bt):
                for j in range(NB):
                    if j == 0:
                        e.wait_ge(s_ix[bt.par], (bt.turn + 1) * 16)
                        e.sem_inc(s_k, 1)
                    if j % 4 == 0:
                        e.wait_ge(s_mm, bt.b * NQ + j // 4 + 1)
                        e.sem_inc(s_k, 1)
                    e.indirect_dma_start(rows[:, bt.par, j, :], None, table,
                                         bass.IndirectOffsetOnAxis(ap=idx[:, bt.par, j:j + 1].bitcast(I32), axis=0)
                                         ).then_inc(s_g[bt.par], 16)
            each_batch(e, U, body)

        @block.scalar
        def _(e):
            def scale(bs, q):
                for j in ACT_TILES[mode]:
                    t = 4 * q + j
                    for h in range(heads):
                        wid = F if heads == 1 else DH
                        g = rows[:, bs.par, t, h * wid:(h + 1) * wid]
                        e.activation(g, g, ACT.Copy, scale=wc[:, bs.par, h, t:t + 1])
                e.wait_ge(s_S, bs.b * NQ + q + 1)
                e.copy(Sb[:, q % NS, :, :], S[:, q % NS, :, :]).then_inc(s_Sb, 1)

            def body(bs, bp):
                if bp is not None:
                    e.wait_ge(s_mm, bp.b * NQ + NQ)
                    e.sem_inc(s_k, 1)
                    e.dma_start(mt[:, bp.par, :, :],
                                d["meta"][bass.ds(bp.b, 1), :, 1:META, :].rearrange("o p c t -> (o p) c t")
                                ).then_inc(s_md[bp.par], 16)
                for k in range(NB):
                    if bs is not None and soft and k % 4 == 1 and k // 4 + 1 < NQ:
                        scale(bs, k // 4 + 1)
                    if bp is not None:
                        prepare(e, "act", k, bp)
                        if mode == "mlp" and k % 4 == 3:
                            q = k // 4
                            e.wait_ge(s_pre, bp.b * NQ + q + 3)
                            g = rows[:, bp.par, 4 * q:4 * q + 4, :]
                            e.activation(g, g, ACT.Gelu).then_inc(s_A, 1)
                if bp is not None and soft:
                    e.wait_ge(s_A, (bp.b + U) * NA + (NA - 1))
                    scale(bp, 0)
            batches(e, U, body)

        @block.tensor
        def _(e):
            e.sem_inc(s_mm, U * NQ)
            e.wait_ge(s_init, 1)
            if mode == "soft1":
                e.matmul(hist[:, :], zb[:, 0:NT], zb[:, 0:P], start=True, stop=False)
            if mode == "mlp":
                e.wait_ge(s_c, 16)

            def expand(bp, qq):
                if soft and qq == 0:
                    e.wait_ge(s_A, (bp.b + U) * NA)
                if not soft:
                    e.wait_ge(s_pre, bp.b * NQ + qq + 1)
                e.wait_ge(s_st, bp.b * NQ + qq + 1 + (NQ if NLRB == 1 else 0))
                e.sem_inc(s_k, 1)
                for i in range(4):
                    t = 4 * qq + i
                    if soft:
                        for part in range(3):
                            last = e.matmul(ex[:, t * heads:(t + 1) * heads], ST[:, qq % 2, i, :],
                                            dw[:, bp.par, t, part * heads:(part + 1) * heads],
                                            start=(part == 0), stop=(part == 2))
                    else:
                        e.matmul(pre[qq % 2][:, i, :], ST[:, qq % 2, i, :], dw[:, bp.par, t, :],
                                 start=True, stop=False)
                        last = e.matmul(pre[qq % 2][:, i, :], wrow[:, bp.par, t * P:(t + 1) * P],
                                        crow[:, :], start=False, stop=True)
                last.then_inc(s_ex, 1)

            def first_ranks(bs, q):
                return load_values(nc, PE, d["rel"][bass.ds(bs.b, 1), 4 * q:4 * q + 4], 3 * P)

            def body(bs, bp):
                if bs is not None:
                    nxt = first_ranks(bs, 0)
                for k in range(NB):
                    q, j = divmod(k, 4)
                    if bp is not None:
                        if mode == "mlp" and j == 0:
                            expand(bp, q)
                        prepare(e, "pe", k, bp)
                    if bs is not None:
                        n = bs.b * NQ + q
                        if j == 0:
                            rel = nxt
                            e.wait_ge(s_Sb if soft else s_S, n + 1)
                            if mode == "soft4":
                                e.wait_ge(s_rs, n + 1)
                            if soft and q == 0:
                                e.wait_ge(s_A, (bs.b + U + 1) * NA)
                            if mode == "mlp":
                                e.wait_ge(s_A, (bs.b + U) * NA + q + 1)
                            e.wait_ge(s_add, n + 1)
                            e.sem_inc(s_k, 1)
                            for i in range(blocks):
                                e.matmul(pn[q % 2][:, i, :], zb[:, 0:P], zb[:, :], start=True, stop=False)
                            if soft:
                                e.matmul(pd[q % 2][:, :], zb[:, 0:3 * heads], zb[:, :], start=True, stop=False)
                        w = bass.ds(rel[j], P)
                        for i in range(blocks):
                            last = e.matmul(pn[q % 2][:, i, w], rows[:, bs.par, k, i * P:(i + 1) * P],
                                            S[:, q % NS, j, :], start=False, stop=(j == 3))
                        if soft:
                            last = e.matmul(pd[q % 2][:, w], w3[:, bs.par, k, :, :].rearrange("p k h -> p (k h)"),
                                            Sb[:, q % NS, j, :], start=False, stop=(j == 3))
                        if mode == "soft1":
                            last = e.matmul(hist[:, :], ho[:, q % NS, j, :], lo[:, q % NS, j, :], start=False, stop=False)
                        if j == 1 and q + 1 < NQ:
                            nxt = first_ranks(bs, q + 1)
                        if j == 3:
                            last.then_inc(s_mm, 1)
                    if mode == "soft4" and bp is not None and k < NQ:
                        expand(bp, k)
            batches(e, U, body)
            if mode == "soft1":
                e.matmul(hist[:, :], zb[:, 0:NT], zb[:, 0:P], start=False, stop=True)

        @block.vector
        def _(e):
            qbase = d["qbase"].rearrange("(o b) q -> o (b q)", o=1)
            e.memset(acc[:, :, :], 0.0)
            e.memset(zb[:, :], 0.0)
            if soft:
                e.memset(den[:, :], 0.0)
                e.memset(I_[:, :, :], -BIG)
                e.memset(RB_[:, :, :], -BIG)
            e.drain().then_inc(s_init, 1)
            e.sem_inc(s_A, U * NA)
            e.sem_inc(s_add, 2)
            if mode == "mlp":
                e.sem_inc(s_pre, 2)
            if dst_w and NLRB == 1:
                e.sem_inc(s_st, NQ)

            def make1(bt, q):
                if q == 0:
                    e.wait_ge(s_md[bt.par], (bt.turn + 1) * 16)
                e.wait_ge(s_mm, bt.b * NQ + (q + U * NQ + 1 - NS))
                if mode == "soft1":
                    sl = slice(4 * q, 4 * q + 4)
                    e.tensor_tensor(ho[:, q % NS, :, :], c["iotab"][:, 0:NT].unsqueeze(1).broadcast_to([P, 4, NT]),
                                    mt[:, bt.par, 2, sl].unsqueeze(2).broadcast_to([P, 4, NT]), ALU.is_equal)

            def make2(bt, q):
                sl = slice(4 * q, 4 * q + 4)
                if mode == "soft1":
                    e.tensor_tensor(lo[:, q % NS, :, :], c["iotab"][:, :].unsqueeze(1).broadcast_to([P, 4, P]),
                                    mt[:, bt.par, 3, sl].unsqueeze(2).broadcast_to([P, 4, P]), ALU.is_equal)
                e.tensor_tensor(S[:, q % NS, :, :], iota[:, :].unsqueeze(1).broadcast_to([P, 4, P]),
                                mt[:, bt.par, 0, sl].unsqueeze(2).broadcast_to([P, 4, P]), ALU.is_equal).then_inc(s_S, 1)

            def scale(bs, q):
                n = 4 - len(ACT_TILES[mode])
                g = rows[:, bs.par, 4 * q:4 * q + n, 0:H * DH].rearrange("p t (h d) -> p t h d", h=H)
                w = wc[:, bs.par, :, 4 * q:4 * q + n].rearrange("p h t -> p t h").unsqueeze(3)
                e.tensor_tensor(g, g, w.broadcast_to([P, n, H, DH]), ALU.mult).then_inc(s_rs, 1)

            def add(n, q, r0):
                e.drain()
                e.wait_ge(s_mm, n + (U * NQ + 1))
                w = acc[:, :, bass.ds(r0, 4 * P)]
                last = e.tensor_tensor(w, w, pn[q % 2][:, :, :], ALU.add)
                if soft:
                    w = den[:, bass.ds(r0, 4 * P)]
                    last = e.tensor_tensor(w, w, pd[q % 2][:, :], ALU.add)
                last.then_inc(s_add, 1)

            def rescale(bs, r0):
                e.drain()
                first = acc[:, :, bass.ds(r0, 1)]
                e.tensor_tensor(first, first, alpha[:, bs.par, :].unsqueeze(2), ALU.mult)
                fd = den[:, bass.ds(r0, 1)]
                e.tensor_tensor(fd, fd, alphad[:, bs.par:bs.par + 1], ALU.mult)

            def body(bs, bp):
                if bs is not None:
                    n = bs.b * NQ
                    if soft:
                        e.wait_ge(s_A, (bs.b + U + 1) * NA)
                    if mode == "soft4":
                        scale(bs, 0)
                for k in range(NB):
                    q, j = divmod(k, 4)
                    bt, nq = (bs, q + 1) if q + 1 < NQ else (bp, 0)
                    if bt is not None and j == 0:
                        make1(bt, nq)
                    if bt is not None and j == 1:
                        make2(bt, nq)
                    if mode == "soft4" and bs is not None and j == 2 and q + 1 < NQ:
                        scale(bs, q + 1)
                    if bp is not None:
                        if dst_w and (k < NQ if soft else k == 0 or (j == 2 and q + 1 < NQ)):
                            for qq in (k if soft else 0 if k == 0 else q + 1,):
                                if qq == 0:
                                    e.wait_ge(s_ld[bp.par], (bp.turn + 1) * (16 * n_ld))
                                if qq >= 2:
                                    e.wait_ge(s_ex, bp.b * NQ + qq - 1)
                                one_hot(e, ST[:, qq % 2, :, :].rearrange("p t e -> p (t e)"),
                                        lrb[:, bp.par % NLRB, qq * 4 * P:(qq + 1) * 4 * P],
                                        c["iotap"][:, 0:1]).then_inc(s_st, 1)
                        if mode == "mlp" and j == 3:
                            if q == 0:
                                e.wait_ge(s_g[bp.par], (bp.turn + 1) * (16 * NB))
                            e.wait_ge(s_ex, bp.b * NQ + q + 1)
                            g = rows[:, bp.par, 4 * q:4 * q + 4, :]
                            e.tensor_tensor(g, g, pre[q % 2][:, :, :], ALU.add).then_inc(s_pre, 1)
                        if mode == "sum" and k == 0:
                            e.wait_ge(s_g[bp.par], (bp.turn + 1) * (16 * NB))
                            e.sem_inc(s_A, 1)
                        prepare(e, "dve", k, bp)
                    if bs is not None and k == 1:
                        if isinstance(bs.b, int) and bs.b == 0:
                            before, r0 = None, load_values(nc, DVE, qbase[:, 0:NQ], N)
                        else:
                            before, *r0 = load_values(nc, DVE, qbase[:, bass.ds(n - 1, NQ + 1)], N)
                    if bs is not None and j == 1:
                        if q > 0:
                            if soft and q == 1:
                                rescale(bs, r0[0])
                            add(n + (q - 1), q - 1, r0[q - 1])
                        elif before is not None:
                            add(n - 1, NQ - 1, before)
                if bp is None:
                    add(n + (NQ - 1), NQ - 1, r0[NQ - 1])
            batches(e, U, body)


ACT_TILES = {"soft1": (0, 1, 2, 3), "soft4": (2, 3), "sum": (), "mlp": ()}


def node_map(nc, sb, hist, c, grank, dinv, rb_d, deg_d, lrn_d):
    with ExitStack() as ctx:
        lrh = sb("nm_lrh", [NT, P], BF16, ctx)
        d, ne, cum, lr, lrm, gr, gm = (sb(f"nm_{n}", [NT, P], F32, ctx)
                                       for n in ("d", "ne", "cum", "lr", "lrm", "gr", "gm"))
        rb, rbi = sb("nm_rb", [NT, 1], F32, ctx), sb("nm_rbi", [NT, 1], I32, ctx)
        off = ctx.enter_context(nc.psum_tensor("nm_off", [P, 512], F32))
        tp = ctx.enter_context(nc.psum_tensor("nm_tp", [P, 2, P], F32))
        dc = sb("nm_dc", [P, NT], F32, ctx)
        s_c, s_o, s_r, s_t, s_d, s_v = (ctx.enter_context(nc.semaphore(f"nm_{n}")) for n in "cortdv")
        s_q = ctx.enter_context(nc.semaphore("nm_q"))
        tri = sb("nm_tri", [P, P], F32, ctx)
        block = ctx.enter_context(nc.Block())

        @block.vector
        def _(e):
            e.tensor_copy(d[:, :], hist[:, :])
            e.tensor_scalar(tri[:, :], c["iota"][:, :], c["iotap"][:, 0:1], None, ALU.is_gt)
            e.drain()
            e.tensor_scalar(ne[:, :], d[:, :], 1.0, None, ALU.min)
            e.drain()
            e.tensor_tensor_scan(cum[:, :], ne[:, :], ne[:, :], 0.0, ALU.add, ALU.max)
            e.drain().then_inc(s_c, 1)
            e.tensor_tensor(lr[:, :], cum[:, :], ne[:, :], ALU.mult)
            e.drain()
            e.tensor_scalar(lrm[:, :], lr[:, :], -1.0, None, ALU.add)
            e.tensor_scalar(lrh[:, :], lr[:, :], -1.0, None, ALU.add)
            e.wait_ge(s_o, 1)
            e.tensor_copy(rbi[:, :], off[0:NT, 0:1])
            e.tensor_copy(rb[:, :], off[0:NT, 0:1])
            e.tensor_scalar(gm[:, :], ne[:, :], -float(1 << 20), float(1 << 20), ALU.mult, ALU.add)
            e.drain()
            e.scalar_tensor_tensor(gr[:, :], lrm[:, :], rb[:, 0:1], gm[:, :], ALU.add, ALU.add)
            e.drain().then_inc(s_r, 1)
            e.wait_ge(s_t, 1)
            e.tensor_scalar(dc[:, :], tp[:, 0, 0:NT], 1.0, None, ALU.add)
            e.tensor_copy(grank[:, :], tp[:, 1, 0:NT])
            e.drain().then_inc(s_v, 1)
            e.wait_ge(s_q, 1)
            e.reciprocal(dinv[:, :], dc[:, :])

        @block.scalar
        def _(e):
            e.wait_ge(s_v, 1)
            e.activation(dc[:, :], dc[:, :], ACT.Sqrt).then_inc(s_q, 1)

        @block.tensor
        def _(e):
            e.wait_ge(s_c, 1)
            e.matmul(off[0:NT, 0:1], tri[0:NT, 0:NT], cum[:, P - 1:P], start=True, stop=True).then_inc(s_o, 1)
            e.wait_ge(s_r, 1)
            for i, t in enumerate((d, gr)):
                last = e.transpose(tp[:, i, 0:NT], t[:, :], c["ident"][0:NT, 0:NT])
            last.then_inc(s_t, 1)

        @block.sync
        def _(e):
            e.wait_ge(s_r, 1)
            e.dma_start(rb_d, rbi[:, :]).then_inc(s_d, 16)
            e.dma_start(deg_d, d[:, :]).then_inc(s_d, 16)
            e.dma_start(lrn_d, lrh[:, :]).then_inc(s_d, 16)
            e.wait_ge(s_d, 48)


def node_pass(nc, sb, layer, acc, den, grank, dinv, c, a, d, out):
    nchain = 2 if layer == 1 else 4
    turns, extra = divmod(NG, nchain)
    blocks, parts, heads = {0: (1, 3, 1), 1: (2, 3 * H, H), 2: (1, 0, 1), 3: (1, 0, 1)}[layer]
    K = blocks * F
    ACTE = mybir.EngineType.Activation
    ident = c["ident"]
    with ExitStack() as ctx:
        def s(name, shape, dt=F32):
            return sb(f"n{layer}_{name}", shape, dt, ctx)

        def ps(name, shape):
            return ctx.enter_context(nc.psum_tensor(f"n{layer}_{name}", shape, F32))

        def sem(name):
            return ctx.enter_context(nc.semaphore(f"n{layer}_{name}"))

        s_held, s_w = c["held"], sem("s_w")
        if layer == 0:
            s_p, s_p2 = sem("s_p"), sem("s_p2")
        if layer == 3:
            s_p2 = sem("s_p2")
        loads = []

        def weight(name, shape, ap):
            t = s(name, shape)
            loads.append((t, ap))
            return t

        if layer == 0:
            wn = weight("wn", [P, H, DH], a["L1_gnn_W_n"].rearrange("h c d -> c h d"))
            wnT = weight("wnT", [DH, H, F], a["WnT"])
            a2 = weight("a2", [DH, 2, H], a["aT"])
            vs = s("vs", [P, 2, H])
            vps = []
        if layer == 1:
            w1 = weight("w1", [P, 2, 2 * F], a["L1_gnn_mlp_W1"].rearrange("(k p) j -> p k j", p=P))
            w2 = weight("w2", [P, 2, F], a["L1_gnn_mlp_W2"].rearrange("(k p) j -> p k j", p=P))
            b1 = weight("b1", [P, 2], a["L1_gnn_mlp_b1"].rearrange("(k p) -> p k", p=P))
            b2 = weight("b2", [P, F], a["L1_gnn_mlp_b2"].rearrange("(o f) -> o f", o=1).broadcast_to([P, F]))
            wg = weight("wg", [P, F], a["L2_gnn_W"])
        if layer == 2:
            b2 = weight("b2", [P, F], a["L2_gnn_b"].rearrange("(o f) -> o f", o=1).broadcast_to([P, F]))
            we = weight("we", [P, 2, F], a["L3_gnn_We1"][0:2 * F, :].rearrange("(k p) j -> p k j", p=P))
            be = weight("be", [P, F], a["L3_gnn_be1"].rearrange("(o f) -> o f", o=1).broadcast_to([P, F]))
        if layer == 3:
            row = lambda n: a[n].rearrange("(o f) -> o f", o=1)
            we2 = weight("we2", [P, F], a["L3_gnn_We2"])
            be2 = weight("be2", [1, F], row("L3_gnn_be2"))
            wu = weight("wu", [P, 2, F], a["L3_gnn_Wu1"].rearrange("(k p) j -> p k j", p=P))
            bu = weight("bu", [P, 1], a["L3_gnn_bu1"].rearrange("(p o) -> p o", o=1))
            wu2 = weight("wu2", [P, F], a["L3_gnn_Wu2"])
            b2 = weight("b2", [P, F], row("L3_gnn_bu2").broadcast_to([P, F]))
            gam = weight("gam", [P, F], row("L3_gnn_gamma").broadcast_to([P, F]))
            bet = weight("bet", [P, F], row("L3_gnn_beta").broadcast_to([P, F]))

        GF = [P, G, F]

        def make_chain(ci):
            n = lambda name, shape, dt=F32: s(f"{name}{ci}", shape, dt)
            sm = sem(f"s_c{ci}")
            s_in, s_out = sem(f"s_in{ci}"), sem(f"s_out{ci}")
            s_sd, s_scat = (sem(f"s_sd{ci}"), sem(f"s_scat{ci}")) if layer in (0, 2) else (None, None)
            xi, y, Es = n("xi", GF), n("y", GF), n("Es", GF)
            x = {0: xi, 3: None}[layer] if layer in (0, 3) else n("x", GF)
            lr = n("lr", [P, G * P], BF16)
            Ar = n("Ar", [P, G, K])
            st6, mv, rs = n("st6", [P, G, 6]), n("mv", [P, G, 2]), n("rs", [P, G, 1])
            pA = ps(f"pA{ci}", [P, blocks, 8, P])
            spare = pA[:, 0, 7, :]
            if layer == 0:
                vps.append(spare[:, 0:2 * H])
            if parts:
                dd, rd = n("dd", [P, G, heads]), n("rd", [P, G, heads])
                pD = spare[:, 0:G * parts].rearrange("p (t k) -> p t k", k=parts)
            stages = []
            S_ = lambda who: (lambda fn: stages.append((who, fn)) or fn)

            tiles_of = lambda t: t.rearrange("(g t p) f -> g p t f", t=G, p=P)[bass.ds(cur["g"], 1)].rearrange("o p t f -> (o p) t f")
            own = n("own", GF) if layer == 2 else None
            dg = n("dg", [1, G * P]) if layer == 3 else None

            n_in = 3 if layer >= 2 else 2
            n_out = 1 if layer == 3 else 2

            def load(e):
                e.dma_start(xi[:, :, :], tiles_of(d["x"])).then_inc(s_in, 16)
                e.dma_start(lr[:, :], d["lrn"].rearrange("(g t) p -> g (t p)", t=G)[bass.ds(cur["g"], 1), :]
                            .broadcast_to([P, G * P])).then_inc(s_in, 16)
                if layer == 2:
                    e.dma_start(own[:, :, :], tiles_of(d["t2"])).then_inc(s_in, 16)
                if layer == 3:
                    e.dma_start(dg[:, :], d["deg"].rearrange("(g t) p -> g (t p)", t=G)[bass.ds(cur["g"], 1), :]).then_inc(s_in, 16)

            win = Ar[:, :, :].rearrange("p t k -> p (t k)").rearrange("p (k t f) -> p k t f", k=blocks, t=G)

            @S_("act")
            def _(e, sem):
                rb = load_values(nc, ACTE, d["rb"].rearrange("(g t) o -> g (o t)", t=G)[bass.ds(cur["g"], 1), :], N)
                for t in range(G):
                    last = e.copy(win[:, :, t, :], acc[:, :, bass.ds(rb[t], P)])
                    if parts:
                        last = e.copy(Es[0:parts, t, :], den[:, bass.ds(rb[t], P)])
                last.then_inc(sem, 1)

            @S_("pe")
            def _(e, sem):
                for t in range(G):
                    for k in range(blocks):
                        last = e.transpose(pA[:, k, t, :], win[:, k, t, :], ident[:, :])
                    if parts:
                        last = e.transpose(pD[:, t, :], Es[0:parts, t, :], ident[0:parts, 0:parts])
                last.then_inc(sem, 1)

            @S_("dve")
            def _(e, sem):
                e.wait_ge(s_in, (cur["turn"] + 1) * (16 * n_in))
                e.sem_inc(s_held, 1)
                e.wait_ge(s_out, cur["turn"] * (16 * n_out) + 1)
                e.sem_inc(s_held, 1)
                last = one_hot(e, Es[:, :, :].rearrange("p t f -> p (t f)"), lr[:, :], c["iotap"][:, 0:1])
                if parts:
                    e.tensor_reduce(dd[:, :, :], pD.rearrange("p t (k h) -> p t h k", k=3), AX.X, ALU.add)
                    e.drain()
                    e.tensor_scalar(dd[:, :, :], dd[:, :, :], 1e-20, None, ALU.max)
                    e.drain()
                    e.reciprocal(rd[:, :, :], dd[:, :, :])
                    e.drain()
                for k in range(blocks):
                    o = Ar[:, :, k * F:(k + 1) * F]
                    if not parts:
                        last = e.tensor_copy(o, pA[:, k, 0:G, :])
                    elif heads == 1:
                        last = e.tensor_tensor(o, pA[:, k, 0:G, :], rd[:, :, :].broadcast_to(GF), ALU.mult)
                    else:
                        for h in range(2):
                            hs = slice(h * DH, (h + 1) * DH)
                            last = e.tensor_tensor(o[:, :, hs], pA[:, k, 0:G, hs],
                                                   rd[:, :, 2 * k + h:2 * k + h + 1].broadcast_to([P, G, DH]), ALU.mult)
                last.then_inc(sem, 1)

            def layernorm(dst, add):
                @S_("dve")
                def _(e, sem):
                    add(e)
                    e.drain()
                    for t in range(G):
                        e.bn_stats(st6[:, t, :], y[:, t, :])
                    e.drain()
                    for t in range(G):
                        e.bn_aggr(mv[:, t, :], st6[:, t, :])
                    e.drain()
                    e.tensor_scalar(rs[:, :, :], mv[:, :, 1:2], 1e-5, None, ALU.add)
                    e.tensor_tensor(y[:, :, :], y[:, :, :], mv[:, :, 0:1].broadcast_to(GF),
                                    ALU.subtract).then_inc(sem, 1)

                @S_("act")
                def _(e, sem):
                    e.activation(rs[:, :, :], rs[:, :, :], ACT.Sqrt).then_inc(sem, 1)

                @S_("dve")
                def _(e, sem):
                    e.reciprocal(rs[:, :, :], rs[:, :, :])
                    e.drain()
                    e.tensor_tensor(dst[:, :, :], y[:, :, :], rs[:, :, :].broadcast_to(GF), ALU.mult).then_inc(sem, 1)

            def update(bias):
                def add(e):
                    e.tensor_tensor(y[:, :, :], xi[:, :, :], pA[:, 0, 0:G, :], ALU.add)
                    if bias is not None:
                        e.drain()
                        e.tensor_tensor(y[:, :, :], y[:, :, :], bias[:, :].unsqueeze(1).broadcast_to(GF), ALU.add)
                return add

            def turned(src, dst, psum):
                @S_("pe")
                def _(e, sem):
                    for t in range(G):
                        last = e.transpose(psum[:, t, :], src[:, t, :], ident[:, :])
                    last.then_inc(sem, 1)

                @S_("act")
                def _(e, sem):
                    e.copy(dst[:, :, :], psum[:, 0:G, :]).then_inc(sem, 1)

            def scattered(src, width, table):
                def scatter(e):
                    for t in range(G):
                        e.indirect_dma_start(table, bass.IndirectOffsetOnAxis(ap=gi[:, t:t + 1], axis=0),
                                             src[:, t, 0:width], None, bounds_check=DRANKS - 1,
                                             oob_is_err=False).then_inc(s_scat, 16)
                    e.wait_ge(s_scat, (cur["turn"] + 1) * (16 * G))
                    e.sem_inc(s_sd, 1)
                return scatter

            def wait_scattered(e):
                e.wait_ge(s_sd, cur["turn"] + 1)
                e.sem_inc(s_held, 1)

            scatter = None
            if layer in (0, 2):
                gi = n("gi", [P, G], I32)
            if layer == 0:
                xT = Es
                tab, sd, sd3 = n("tab", [P, G, W1]), n("sd", [P, G, H]), n("sd3", [P, G, 3, H], BF16)

                @S_("pe")
                def _(e, sem):
                    for t in range(G):
                        last = e.matmul(pA[:, 0, t, :], Es[:, t, :], Ar[:, t, :], start=True, stop=True)
                    last.then_inc(sem, 1)

                layernorm(x, update(None))
                turned(x, xT, pA[:, 0])
                pairs = pA[:, 0, :, :].rearrange("p (a b) c -> p a (b c)", b=2)
                for t0 in range(0, G, 3):
                    tiles = range(t0, min(t0 + 3, G))

                    @S_("pe")
                    def _(e, sem, tiles=tiles):
                        for t in tiles:
                            last = e.matmul(pairs[:, t % 3, :], xT[:, t, :], wn[:, :, :].rearrange("p h d -> p (h d)"),
                                            start=True, stop=True)
                        if tiles[0] == 0:
                            for t in range(G):
                                last = e.matmul(spare[:, 2 * H * t:2 * H * (t + 1)], xT[:, t, :],
                                                vs[:, :, :].rearrange("p k h -> p (k h)"), start=True, stop=True)
                        last.then_inc(sem, 1)

                    @S_("act")
                    def _(e, sem, tiles=tiles):
                        last = e.copy(tab[:, tiles[0]:tiles[-1] + 1, 0:H * DH], pairs[:, 0:len(tiles), :])
                        last.then_inc(sem, 1)

                @S_("dve")
                def _(e, sem):
                    scores = spare[:, 0:G * 2 * H].rearrange("p (t k) -> p t k", t=G)
                    wait_scattered(e)
                    e.tensor_copy(tab[:, :, H * DH:W1], scores[:, :, 0:H])
                    e.tensor_copy(sd[:, :, :], scores[:, :, H:2 * H])
                    e.tensor_copy(gi[:, :], grank[:, bass.ds(cur["g"] * G, G)])
                    e.drain()
                    e.tensor_copy(sd3[:, :, 0, :], sd[:, :, :])
                    for part in (1, 2):
                        e.drain()
                        e.tensor_tensor(sd[:, :, :], sd[:, :, :], sd3[:, :, part - 1, :], ALU.subtract)
                        e.drain()
                        last = e.tensor_copy(sd3[:, :, part, :], sd[:, :, :])
                    last.then_inc(sem, 1)

                outs = ((d["x"], x), (d["t1"], tab))
                scatter = scattered(sd3[:, :, :, :].rearrange("p t k h -> p t (k h)"), 3 * H, d["sd"])
            if layer == 1:
                cc = Ar
                ccT = [t[:, :, :].rearrange("p t f -> p (t f)") for t in (y, Es)]
                hid = Ar[:, :, :].rearrange("p t k -> p (t k)").rearrange("p (k n) -> p k n", k=2)
                xT = Es

                @S_("pe")
                def _(e, sem):
                    for t in range(G):
                        for k in range(2):
                            last = e.matmul(pA[:, k, t, :], Es[:, t, :], Ar[:, t, k * F:(k + 1) * F], start=True, stop=True)
                    last.then_inc(sem, 1)

                @S_("act")
                def _(e, sem):
                    for k in range(2):
                        last = e.activation(cc[:, :, k * F:(k + 1) * F], pA[:, k, 0:G, :], ACT.Relu)
                    last.then_inc(sem, 1)

                @S_("pe")
                def _(e, sem):
                    for t in range(G):
                        for k in range(2):
                            last = e.transpose(pA[:, k, t, :], cc[:, t, k * F:(k + 1) * F], ident[:, :])
                    last.then_inc(sem, 1)

                @S_("act")
                def _(e, sem):
                    for k in range(2):
                        last = e.copy(ccT[k], pA[:, k, 0:G, :].rearrange("p t f -> p (t f)"))
                    last.then_inc(sem, 1)

                @S_("pe")
                def _(e, sem):
                    for j in range(2):
                        o = pA[:, j].rearrange("p t f -> p (t f)")
                        for lo_, hi_ in ((0, 4 * P), (4 * P, G * P)):
                            for k in range(2):
                                last = e.matmul(o[:, lo_:hi_], w1[:, k, j * F:(j + 1) * F], ccT[k][:, lo_:hi_],
                                                start=(k == 0), stop=(k == 1))
                    last.then_inc(sem, 1)

                @S_("act")
                def _(e, sem):
                    for j in range(2):
                        last = e.activation(hid[:, j, :], pA[:, j, 0:G, :].rearrange("p t f -> p (t f)"), ACT.Relu,
                                            bias=b1[:, j:j + 1])
                    last.then_inc(sem, 1)

                @S_("pe")
                def _(e, sem):
                    for t in range(G):
                        for j in range(2):
                            last = e.matmul(pA[:, 0, t, :], hid[:, j, t * P:(t + 1) * P], w2[:, j, :],
                                            start=(j == 0), stop=(j == 1))
                    last.then_inc(sem, 1)

                layernorm(x, update(b2))
                turned(x, xT, pA[:, 1])

                @S_("pe")
                def _(e, sem):
                    for t in range(G):
                        last = e.matmul(pA[:, 0, t, :], xT[:, t, :], wg[:, :], start=True, stop=True)
                    last.then_inc(sem, 1)

                @S_("dve")
                def _(e, sem):
                    e.tensor_tensor(y[:, :, :], pA[:, 0, 0:G, :],
                                    dinv[:, bass.ds(cur["g"] * G, G)].unsqueeze(2).broadcast_to(GF),
                                    ALU.mult).then_inc(sem, 1)

                outs = ((d["x"], x), (d["t2"], y))
            if layer == 2:
                xT, ta = Es, y
                tb = n("tb", GF)

                @S_("pe")
                def _(e, sem):
                    for t in range(G):
                        last = e.matmul(pA[:, 0, t, :], Es[:, t, :], Ar[:, t, :], start=True, stop=True)
                    last.then_inc(sem, 1)

                @S_("dve")
                def _(e, sem):
                    e.tensor_tensor(y[:, :, :], own[:, :, :], pA[:, 0, 0:G, :], ALU.add)
                    e.drain()
                    e.tensor_tensor(y[:, :, :], y[:, :, :],
                                    dinv[:, bass.ds(cur["g"] * G, G)].unsqueeze(2).broadcast_to(GF), ALU.mult)
                    e.drain()
                    e.tensor_tensor(y[:, :, :], y[:, :, :], b2[:, :].unsqueeze(1).broadcast_to(GF), ALU.add).then_inc(sem, 1)

                @S_("act")
                def _(e, sem):
                    e.activation(y[:, :, :], y[:, :, :], ACT.Gelu).then_inc(sem, 1)

                layernorm(x, lambda e: e.tensor_tensor(y[:, :, :], xi[:, :, :], y[:, :, :], ALU.add))
                turned(x, xT, pA[:, 0])

                for k in range(2):
                    @S_("pe")
                    def _(e, sem, k=k):
                        for t in range(G):
                            last = e.matmul(pA[:, 0, t, :], xT[:, t, :], we[:, k, :], start=True, stop=True)
                        last.then_inc(sem, 1)
                    if k == 0:
                        @S_("act")
                        def _(e, sem):
                            e.copy(ta[:, :, :], pA[:, 0, 0:G, :]).then_inc(sem, 1)

                @S_("dve")
                def _(e, sem):
                    wait_scattered(e)
                    e.tensor_tensor(tb[:, :, :], pA[:, 0, 0:G, :], be[:, :].unsqueeze(1).broadcast_to(GF), ALU.add)
                    e.tensor_copy(gi[:, :], grank[:, bass.ds(cur["g"] * G, G)]).then_inc(sem, 1)

                outs = ((d["x"], x), (d["t3"], ta))
                scatter = scattered(tb, F, d["bd"])
            if layer == 3:
                flat = lambda t: t.rearrange("p t f -> p (t f)")
                aT, xT, mT = n("aT", GF), n("xT", GF), Ar
                uT = Es
                halves = ((0, 4 * P), (4 * P, G * P))

                turned(xi, xT, pA[:, 0])

                @S_("pe")
                def _(e, sem):
                    for t in range(G):
                        last = e.matmul(pA[:, 0, t, :], Ar[:, t, :], Es[:, t, :], start=True, stop=True)
                    last.then_inc(sem, 1)

                @S_("act")
                def _(e, sem):
                    e.copy(aT[:, :, :], pA[:, 0, 0:G, :]).then_inc(sem, 1)

                @S_("pe")
                def _(e, sem):
                    for lo_, hi_ in halves:
                        o = flat(pA[:, 0])[:, lo_:hi_]
                        e.matmul(o, we2[:, :], flat(aT[:, :, :])[:, lo_:hi_], start=True, stop=False)
                        last = e.matmul(o, be2[:, :], dg[:, lo_:hi_], start=False, stop=True)
                    last.then_inc(sem, 1)

                @S_("act")
                def _(e, sem):
                    e.copy(mT[:, :, :], pA[:, 0, 0:G, :]).then_inc(sem, 1)

                @S_("pe")
                def _(e, sem):
                    for lo_, hi_ in halves:
                        o = flat(pA[:, 0])[:, lo_:hi_]
                        e.matmul(o, wu[:, 0, :], flat(xT[:, :, :])[:, lo_:hi_], start=True, stop=False)
                        last = e.matmul(o, wu[:, 1, :], flat(mT[:, :, :])[:, lo_:hi_], start=False, stop=True)
                    last.then_inc(sem, 1)

                @S_("act")
                def _(e, sem):
                    e.activation(uT[:, :, :], pA[:, 0, 0:G, :], ACT.Gelu, bias=bu[:, 0:1]).then_inc(sem, 1)

                @S_("pe")
                def _(e, sem):
                    for t in range(G):
                        last = e.matmul(pA[:, 0, t, :], uT[:, t, :], wu2[:, :], start=True, stop=True)
                    last.then_inc(sem, 1)

                layernorm(y, update(b2))

                def scaled(e):
                    e.tensor_tensor(y[:, :, :], y[:, :, :], gam[:, :].unsqueeze(1).broadcast_to(GF), ALU.mult)
                    e.drain()
                    e.tensor_tensor(y[:, :, :], y[:, :, :], bet[:, :].unsqueeze(1).broadcast_to(GF), ALU.add)
                    e.drain()
                    e.tensor_tensor(y[:, :, :], y[:, :, :], xi[:, :, :], ALU.add)
                layernorm(y, scaled)

                outs = ((out, y),)

            def store(e):
                for table, rows in outs:
                    if table is not out:
                        e.dma_start(tiles_of(table), rows[:, :, :]).then_inc(s_out, 16)
                    elif isinstance(cur["g"], int) and cur["g"] == NG - 1:
                        whole = N - NLAST
                        e.dma_start(out[whole - (G - 1) * P:whole, :].rearrange("(t p) f -> p t f", p=P),
                                    rows[:, 0:G - 1, :]).then_inc(s_out, 16)
                        e.dma_start(out[whole:N, :], rows[0:NLAST, G - 1, :]).then_inc(s_p2, 16)
                    else:
                        e.dma_start(tiles_of(out[0:(NG - 1) * G * P, :]), rows[:, :, :]).then_inc(s_out, 16)
            return Chain(ci, stages, sm, load, store, 16 * n_out, s_out, scatter, s_sd)

        cur = {}
        chains = [make_chain(ci) for ci in range(nchain)]
        block = ctx.enter_context(nc.Block())

        def run(e, turn):
            with e.Fori(0, turns) as it:
                turn(it, chains)
            turn(turns, chains[:extra])

        def take(ch, it):
            cur["g"], cur["turn"] = it * nchain + ch.ci, it

        def compute(e, name):
            def turn(it, active):
                for k in range(len(chains[0].stages)):
                    for ch in active:
                        take(ch, it)
                        one_stage(e, name, ch.stages, k, it, ch.done, s_held)
            run(e, turn)

        @block.sync
        def _(e):
            for t, ap in loads:
                e.dma_start(t.ap(), ap, allow_slow_non_contiguous=True).then_inc(s_w, 16)
            e.wait_ge(s_w, 16 * len(loads))
            if layer == 0:
                e.wait_ge(s_p2, 1)
            for ch in chains:
                e.sem_inc(ch.s_out, 1)
                if ch.scatter:
                    e.sem_inc(ch.s_sd, 1)
                e.sem_inc(ch.done, 1)

            def turn(it, active):
                for ch in active:
                    take(ch, it)
                    if layer == 0:
                        e.wait_ge(ch.s_out, it * ch.w_out + 1)
                    ch.load(e)
                for ch in active:
                    take(ch, it)
                    e.wait_ge(ch.done, (it + 1) * len(ch.stages) + 1)
                    ch.store(e)
            run(e, turn)
            for ch in chains:
                e.wait_ge(ch.s_out, (turns + (ch.ci < extra)) * ch.w_out + 1)
                if ch.scatter:
                    e.wait_ge(ch.s_sd, turns + (ch.ci < extra) + 1)
            if layer == 3:
                e.wait_ge(s_p2, 16)

        @block.tensor
        def _(e):
            if layer == 0:
                e.wait_ge(s_w, 16 * len(loads))
                for h in range(H):
                    for k in range(2):
                        last = e.matmul(vps[0][:, k * H + h:k * H + h + 1], wnT[:, h, :], a2[:, k, h:h + 1],
                                        start=True, stop=True)
                last.then_inc(s_p, 1)
            compute(e, "pe")

        @block.vector
        def _(e):
            if layer == 0:
                e.wait_ge(s_p, 1)
                e.tensor_copy(vs[:, :, :].rearrange("p k h -> p (k h)"), vps[0]).then_inc(s_p2, 1)
            compute(e, "dve")

        @block.scalar
        def _(e):
            compute(e, "act")

        if layer in (0, 2):
            @block.gpsimd
            def _(e):
                def turn(it, active):
                    for ch in active:
                        take(ch, it)
                        e.wait_ge(ch.done, (it + 1) * len(ch.stages) + 1)
                        e.sem_inc(s_held, 1)
                        ch.scatter(e)
                run(e, turn)


class Chain:

    def __init__(self, ci, stages, done, load, store, w_out, s_out, scatter, s_sd):
        self.ci, self.stages, self.done, self.load, self.store = ci, stages, done, load, store
        self.w_out, self.s_out, self.scatter, self.s_sd = w_out, s_out, scatter, s_sd


def one_stage(eng, name, stages, k, turn, done, held):
    if stages[k][0] != name:
        return
    eng.wait_ge(done, turn * len(stages) + k + 1)
    eng.sem_inc(held, 1)
    stages[k][1](eng, done)


_INS = ["x", "src", "dst", "edge_weight", "L0_gnn_W", "L1_gnn_W_n", "L1_gnn_a_src", "L1_gnn_a_dst",
        "L1_gnn_mlp_W1", "L1_gnn_mlp_b1", "L1_gnn_mlp_W2", "L1_gnn_mlp_b2", "L2_gnn_W", "L2_gnn_b",
        "L3_gnn_We1", "L3_gnn_be1", "L3_gnn_We2", "L3_gnn_be2", "L3_gnn_Wu1", "L3_gnn_bu1", "L3_gnn_Wu2",
        "L3_gnn_bu2", "L3_gnn_gamma", "L3_gnn_beta"]


def kernel(**inputs):
    import numpy as np
    import concourse.bacc as bacc
    from concourse.bass_utils import run_bass_kernel_spmd

    nc = bacc.Bacc("TRN2", target_bir_lowering=False, num_devices=1)
    arrays, a = {}, {}
    for name in _INS:
        v = np.ascontiguousarray(inputs[name])
        arrays[f"in_{name}"] = v
        a[name] = nc.dram_tensor(f"in_{name}", v.shape, mybir.dt.from_np(v.dtype), kind="ExternalInput").ap()
    wt = np.ascontiguousarray(np.transpose(np.asarray(inputs["L1_gnn_W_n"]), (2, 0, 1)))
    arrays["in_WnT"] = wt
    a["WnT"] = nc.dram_tensor("in_WnT", wt.shape, F32, kind="ExternalInput").ap()
    at = np.ascontiguousarray(np.transpose(np.stack([np.asarray(inputs["L1_gnn_a_src"]),
                                                     np.asarray(inputs["L1_gnn_a_dst"])]), (2, 0, 1)))
    arrays["in_aT"] = at
    a["aT"] = nc.dram_tensor("in_aT", at.shape, F32, kind="ExternalInput").ap()
    out = nc.dram_tensor("out_0", (N, F), F32, kind="ExternalOutput").ap()
    prog(nc, a, out)
    r = run_bass_kernel_spmd(nc, [arrays], core_ids=[0])
    return r.results[0]["out_0"]
```
